# Optimizing a Trainium2 kernel written in Bass

```python
import numpy as np
import jax
import jax.numpy as jnp

def _softmax(x, axis=-1):
    return jax.nn.softmax(x, axis=axis)

def _gelu(x):
    return jax.nn.gelu(x, approximate=True)

def _silu(x):
    return jax.nn.silu(x)

def _sigmoid(x):
    return jax.nn.sigmoid(x)

def _layernorm(x, axis=-1, eps=1e-05):
    m = jnp.mean(x, axis=axis, keepdims=True)
    v = jnp.var(x, axis=axis, keepdims=True)
    return (x - m) / jnp.sqrt(v + eps)

def _scatter_add(tgt, idx, src, axis=0):
    return tgt.at[idx].add(src)

def _segment_sum(src, seg, n):
    return jax.ops.segment_sum(src, seg, n)
kernel_name = 'mk_xattn_ffn_d1_seqx_r8_118266'

def setup_inputs(seed: int=0):
    np.random.seed(seed)
    _w = jnp.asarray

    def _rec_inputs():
        import jax
        import jax.numpy as jnp
        _rk = jax.random.key(seed)
        x = 7.22e-05 + 1 * jax.random.normal(jax.random.fold_in(_rk, 1), (4, 512, 128), jnp.float32)
        _lenS = 512 - jax.random.randint(jax.random.fold_in(_rk, 7), (4,), 0, max(1, 512 // 4) + 1, jnp.int32)
        _lenS2 = 77 - jax.random.randint(jax.random.fold_in(_rk, 8), (4,), 0, max(1, 77 // 4) + 1, jnp.int32)
        _ctx_1024P = jax.random.normal(jax.random.fold_in(_rk, 11), (4, 16, 128), jnp.float32)
        _ctx_1024c = jax.random.dirichlet(jax.random.fold_in(_rk, 511), 0.3 * jnp.ones((16,), jnp.float32), (4, 77))
        _ctx_1024t = jnp.einsum('bsk,bkd->bsd', _ctx_1024c, _ctx_1024P)
        _ctx_1024t = _ctx_1024t * jax.lax.rsqrt(jnp.mean(jnp.square(_ctx_1024t)) + 1e-12) * 0.953939
        ctx_1024 = 4.13588e-05 + 0.999923 * (_ctx_1024t + 0.3 * jax.random.normal(jax.random.fold_in(_rk, 611), (4, 77, 128), jnp.float32))
        return (x, ctx_1024)
    x, ctx_1024 = _rec_inputs()

    def _L0_xattn_setup():
        import jax, jax.numpy as jnp
        import numpy as np
        B, NQ, NK = (4, 256, 256)
        QDIM = CDIM = 128
        H, DH = (16, 64)
        SCALE = DH ** (-0.5)
        WSTD = 0.02
        key = jax.random.key(seed)
        ks = jax.random.split(key, 6)
        inner = H * DH
        return {'x': jax.random.normal(ks[0], (B, NQ, QDIM), dtype=jnp.float32), 'context': jax.random.normal(ks[1], (B, NK, CDIM), dtype=jnp.float32), 'Wq': jax.random.normal(ks[2], (inner, QDIM), dtype=jnp.float32) * WSTD, 'Wk': jax.random.normal(ks[3], (inner, CDIM), dtype=jnp.float32) * WSTD, 'Wv': jax.random.normal(ks[4], (inner, CDIM), dtype=jnp.float32) * WSTD, 'Wo': jax.random.normal(ks[5], (QDIM, inner), dtype=jnp.float32) * WSTD, 'bo': jnp.zeros((QDIM,), dtype=jnp.float32)}
    _L0_xattn_all = _L0_xattn_setup()
    _L0_xattn_in = {k: v for k, v in _L0_xattn_all.items() if k in ('Wq', 'Wk', 'Wv', 'Wo', 'bo')}
    del _L0_xattn_all

    def _L0_ffn_setup():
        import jax, jax.numpy as jnp
        import numpy as np
        N_EMBD = 128
        NUM_EXPERTS = 8
        TOP_K = 2
        D_FF = 4 * N_EMBD
        B, S = (4, 256)
        key = jax.random.key(seed)
        ks = jax.random.split(key, 7)
        scale = lambda fan_in: 1.0 / np.sqrt(fan_in)
        x = jax.random.normal(ks[0], (B, S, N_EMBD), dtype=jnp.float32)
        W_router = jax.random.normal(ks[1], (N_EMBD, NUM_EXPERTS), dtype=jnp.float32) * scale(N_EMBD)
        b_router = jnp.zeros((NUM_EXPERTS,), dtype=jnp.float32)
        W1 = jax.random.normal(ks[2], (NUM_EXPERTS, N_EMBD, D_FF), dtype=jnp.float32) * scale(N_EMBD)
        b1 = jnp.zeros((NUM_EXPERTS, D_FF), dtype=jnp.float32)
        W2 = jax.random.normal(ks[3], (NUM_EXPERTS, D_FF, N_EMBD), dtype=jnp.float32) * scale(D_FF)
        b2 = jnpp = jnp.zeros((NUM_EXPERTS, N_EMBD), dtype=jnp.float32)
        return {'x': x, 'W_router': W_router, 'b_router': b_router, 'W1': W1, 'b1': b1, 'W2': W2, 'b2': b2}
    _L0_ffn_all = _L0_ffn_setup()
    _L0_ffn_in = {k: v for k, v in _L0_ffn_all.items() if k in ('W_router', 'b_router', 'W1', 'b1', 'W2', 'b2')}
    del _L0_ffn_all
    return {'x': x, 'ctx_1024': ctx_1024, 'L0_xattn_Wq': _L0_xattn_in['Wq'], 'L0_xattn_Wk': _L0_xattn_in['Wk'], 'L0_xattn_Wv': _L0_xattn_in['Wv'], 'L0_xattn_Wo': _L0_xattn_in['Wo'], 'L0_xattn_bo': _L0_xattn_in['bo'], 'L0_ffn_W_router': _L0_ffn_in['W_router'], 'L0_ffn_b_router': _L0_ffn_in['b_router'], 'L0_ffn_W1': _L0_ffn_in['W1'], 'L0_ffn_b1': _L0_ffn_in['b1'], 'L0_ffn_W2': _L0_ffn_in['W2'], 'L0_ffn_b2': _L0_ffn_in['b2']}

def reference(x, ctx_1024, L0_xattn_Wq, L0_xattn_Wk, L0_xattn_Wv, L0_xattn_Wo, L0_xattn_bo, L0_ffn_W_router, L0_ffn_b_router, L0_ffn_W1, L0_ffn_b1, L0_ffn_W2, L0_ffn_b2):
    import jax
    import jax.numpy as jnp

    def _L0_xattn_ref(x, context, Wq, Wk, Wv, Wo, bo):
        import jax, jax.numpy as jnp
        import numpy as np
        B, NQ, NK = (4, 256, 256)
        QDIM = CDIM = 128
        H, DH = (16, 64)
        SCALE = DH ** (-0.5)
        WSTD = 0.02
        b, nq, _ = x.shape
        nk = context.shape[1]
        q = (x @ Wq.T).reshape(b, nq, H, DH)
        k = (context @ Wk.T).reshape(b, nk, H, DH)
        v = (context @ Wv.T).reshape(b, nk, H, DH)
        sim = jnp.einsum('bihd,bjhd->bhij', q, k) * SCALE
        attn = jax.nn.softmax(sim, axis=-1)
        out = jnp.einsum('bhij,bjhd->bihd', attn, v).reshape(b, nq, H * DH)
        return out @ Wo.T + bo

    def _L0_ffn_ref(x, W_router, b_router, W1, b1, W2, b2):
        import jax, jax.numpy as jnp
        import numpy as np
        N_EMBD = 128
        NUM_EXPERTS = 8
        TOP_K = 2
        D_FF = 4 * N_EMBD
        B, S = (4, 256)
        Bv, Sv, D = x.shape
        flat_x = x.reshape(-1, D)
        T = flat_x.shape[0]
        logits = flat_x @ W_router + b_router
        top_vals, top_idx = jax.lax.top_k(logits, TOP_K)
        neg_inf = jnp.full_like(logits, -jnp.inf)
        sparse_logits = neg_inf.at[jnp.arange(T)[:, None], top_idx].set(top_vals)
        router_weights = jax.nn.softmax(sparse_logits, axis=-1)
        final_output = jnp.zeros_like(flat_x)
        for e in range(NUM_EXPERTS):
            expert_mask = jnp.any(top_idx == e, axis=-1)
            h = jax.nn.relu(flat_x @ W1[e] + b1[e])
            y = h @ W2[e] + b2[e]
            w = router_weights[:, e] * expert_mask.astype(x.dtype)
            final_output = final_output + y * w[:, None]
        return final_output.reshape(Bv, Sv, D)
    x = x + _L0_xattn_ref(_layernorm(x, axis=-1), ctx_1024, L0_xattn_Wq, L0_xattn_Wk, L0_xattn_Wv, L0_xattn_Wo, L0_xattn_bo)
    x = x + _L0_ffn_ref(_layernorm(x, axis=-1), L0_ffn_W_router, L0_ffn_b_router, L0_ffn_W1, L0_ffn_b1, L0_ffn_W2, L0_ffn_b2)
    return x

_drawn_inputs = setup_inputs


def setup_inputs(seed=0):
    import zlib

    import numpy as np

    out = dict(_drawn_inputs(seed))
    spreads = {'L0_xattn_bo': (0.0, 0.1),
     'L0_ffn_b_router': (0.0, 0.1),
     'L0_ffn_b1': (0.0, 0.1),
     'L0_ffn_b2': (0.0, 0.1)}
    factors = {'L0_xattn_Wq': 4.093, 'L0_xattn_Wk': 4.397}
    for name, (base, spread) in spreads.items():
        noise = np.random.default_rng([zlib.crc32(name.encode()), seed]).standard_normal(out[name].shape)
        drawn = base * np.exp(spread * noise) if base else spread * noise
        out[name] = jnp.asarray(drawn.astype(out[name].dtype))
    for name, factor in factors.items():
        out[name] = (out[name] * factor).astype(out[name].dtype)
    return out
```

```python
from contextlib import ExitStack

import concourse.bass as bass
from concourse import mybir

P = 128
ALU = mybir.AluOpType
ACT = mybir.ActivationFunctionType
F32 = mybir.dt.float32
R32 = mybir.dt.float32r
AX_X = mybir.AxisListType.X

NB, NQ, D = 4, 512, 128
NK = 77
H, DH = 16, 64
NE, FF = 8, 512
EPS = 1e-5
BELOW_ALL = -1e38
SCALE = DH ** -0.5

NT = NQ // P
HJ = H * NK
NC = -(-HJ // P)
HJP = NC * P
FB = FF // P
NU = NE * FB
BANK = 512

SC, TR, PV, HP, YP = 0, 2, 3, 4, 6
NS = 2 * NT
HS = H // 2
SW = HS * NK
GROUPS = ((0, 4), (4, 8), (8, NC))
FOLDS = 8 + H + NB * len(GROUPS)

LAG = 3
SLOTS = NU + LAG + 1
MAIN = {
    "scores": (-1, -1, 4, 8, 10, 12, 14, 17),
    "shift": (-1, 0, 4, 8, 10, 13, 15, 18),
    "exp": (1, 2, 6, 11, 12, 15, 15, 19),
    "sum": (2, 2, 5, 10, 11, 15, 17, 19),
    "turn": (4, 6, 9, 12, 13, 14, 18, 19, 21, 25, 26, 27),
    "project": (16, 28),
    "add": (15, 27),
    "back": (16, 30),
    "ln2": (16, 29),
    "ln1": (18,),
    "turn1": (23,),
    "split_a": (18,),
    "split_v": (0,),
    "top2": (0,),
    "turn_w": (3,),
    "spread": (5, 7, 11, 19, 20, 26, 28, 32),
    "max": (-1, -1, 3, 7, 9, 12, 14, 18),
    "turn_hi": (4, 6, 9, 12, 13, 14, 18, 19, 21, 25, 26, 26),
    "turn_lo": (3, 6, 9, 12, 13, 13, 18, 19, 21, 25, 26, 26),
    "weight": (5, 10, 15, 19, 23, 27, 30, 35),
}
FIRST = {
    "scores": (0, 1, 2, 5, 8, 10, 12, 15),
    "shift": (0, 1, 4, 6, 8, 10, 13, 16),
    "exp": (0, 3, 4, 6, 9, 11, 14, 17),
    "sum": (0, 1, 5, 7, 10, 12, 15, 18),
    "turn": (3, 6, 7, 9, 11, 14, 15, 16, 18, 20, 20, 20),
    "project": (15, 21),
    "add": (15, 23),
    "back": (16, 25),
    "ln2": (17, 28),
    "ln1": (18,),
    "turn1": (19,),
    "split_a": (17,),
    "split_v": (13,),
    "max": (0, 1, 2, 5, 8, 10, 13, 16),
    "turn_hi": (4, 6, 7, 9, 11, 12, 15, 16, 19, 22, 23, 24),
    "turn_lo": (4, 6, 7, 9, 11, 12, 15, 15, 18, 20, 20, 20),
    "fold": (2, 4, 2, 3, 4, 2, 3, 4, 2, 2, 5, 2, 1),
    "experts": (8, 8, 10, 14, 18, 18, 18, 21),
}


def need(eng, sem, count):
    if isinstance(count, int) and count <= 0:
        return
    eng.wait_ge(sem, count)


def steps_at(table, what, q):
    return [n for n, at in enumerate(table.get(what, ())) if at == q]


def folds_at(table, q):
    counts = table.get("fold", ())
    return range(sum(counts[:q]), sum(counts[:q + 1])) if q < len(counts) else ()


def xattn_moe_kernel(nc, x_nat, x_t, ctx_t, w_attn, w1, w2, vecs, consts, sel, out):
    with ExitStack() as ctx:
        place = [-(-nc.sbuf_base // 32) * 32]

        def at(name, shape, dt, offset):
            return nc.alloc_sbuf_tensor_at(name, shape, dt, offset=offset)

        def sb(name, shape, dt=F32):
            size = 4
            for n in shape[1:]:
                size *= n
            here = place[0]
            place[0] += -(-size // 32) * 32
            assert place[0] <= nc.sbuf_usable_end, (name, place[0], nc.sbuf_usable_end)
            return at(name, shape, dt, here)

        def offset():
            return place[0]

        w_hi_at = offset()
        w_hi = sb("w_hi", [P, NE * 2 * FF], R32)
        w_lo_at = offset()
        w_lo = sb("w_lo", [P, NE * 2 * FF], R32)
        later = 4 * 3 * 2 * FF
        k_t = at("k_t", [P, 8, NB * NK], F32, w_hi_at + later)
        v_t = at("v_t", [P, 8, NB * NK], F32, w_hi_at + later + 4 * 8 * NB * NK)
        vwt = at("vwt", [P, NB, HJP], F32, w_lo_at + later)
        a_all = sb("a_all", [P, NB * HJ])
        a_hi = sb("a_hi", [P, HJ], R32)
        a_lo = sb("a_lo", [P, HJ], R32)
        vw_all = sb("vw_all", [P, NB * HJP])
        vw_hi = sb("vw_hi", [P, HJP], R32)
        vw_lo = sb("vw_lo", [P, HJP], R32)
        pt_hi = sb("pt_hi", [P, NC, 2 * P], R32)
        pt_lo = sb("pt_lo", [P, NC, 2 * P], R32)
        h_at = offset()
        h_hi = sb("h_hi", [P, 4, NQ], R32)
        h_lo = sb("h_lo", [P, 4, NQ], R32)
        raw = at("raw", [P, 4, 2 * FF], F32, h_at)
        h32 = sb("h32", [P, 2, NQ])
        ytmp_at = offset()
        ytmp = sb("ytmp", [P, 2, NQ])
        sel_raw = at("sel_raw", [2 * NE, NE * P], F32, ytmp_at)
        e_sb = sb("e_sb", [P, 2, HJP])
        xn1 = sb("xn1", [P, NT, D])
        xn2 = sb("xn2", [P, NT, D])
        x1_hi = sb("x1_hi", [P, NQ], R32)
        x1_lo = sb("x1_lo", [P, NQ], R32)
        x2_hi = sb("x2_hi", [P, NQ], R32)
        x2_lo = sb("x2_lo", [P, NQ], R32)
        xin = sb("xin", [P, NT, D])
        x2t = sb("x2t", [P, NQ])
        acc_at = offset()
        acc = sb("acc", [P, NQ])
        ctx_sb = at("ctx_sb", [P, NB * NK], F32, acc_at)
        wb = sb("wb", [P, 2, NQ])
        sel_r = sb("sel_r", [2 * NE, NE * P], R32)
        wt_r = sb("wt_r", [2 * NE, NQ], R32)
        con = sb("con", [P, P + NE + NT])
        vec = sb("vec", [P, NU + NE + 1 + 2 * NE])
        wr_hi, wr_lo = sb("wr_hi", [P, NE], R32), sb("wr_lo", [P, NE], R32)
        mx, ssum, rinv = sb("mx", [P, 2, HS]), sb("ssum", [P, 2, HS]), sb("rinv", [P, 2, HS])

        def statistics(k):
            return {n: sb(f"{n}{k}", [P, NT] + ([6] if n == "stats" else []))
                    for n in ("stats", "mean", "m_sum", "m_dif", "var_in", "var_between", "var", "rstd")}

        ln1, ln2 = statistics(1), statistics(2)
        lg, lg2 = sb("lg", [P, NT, NE]), sb("lg2", [P, NT, NE])
        best, place_of = sb("best", [P, 2, NT]), sb("place_of", [P, 2, NT])
        gap, egap = sb("gap", [P, NT]), sb("egap", [P, NT])
        den, p1, p2 = sb("den", [P, NT]), sb("p1", [P, NT]), sb("p2", [P, NT])
        is1, is2 = sb("is1", [P, NT, NE]), sb("is2", [P, NT, NE])
        rw, rw_r = sb("rw", [P, NT, NE]), sb("rw_r", [P, NT, NE], R32)
        w16 = sb("w16", [P, NT, 2 * NE])

        ident, rank, minus_half = con[:, 0:P], con[:, P:P + NE], con[:, P + NE:P + NE + NT]
        b1_v, b2_v, bo_v = vec[:, 0:NU], vec[:, NU:NU + NE], vec[:, NU + NE:NU + NE + 1]
        br_v = vec[:, NU + NE + 1:NU + 2 * NE + 1]
        wr_v = vec[:, NU + 2 * NE + 1:NU + 3 * NE + 1]

        ps = ctx.enter_context(nc.psum_tensor("ps", [P, 8, BANK], F32))

        def sem(name):
            return ctx.enter_context(nc.semaphore(name))

        in_con, in_vec, in_sel, in_ctx = sem("in_con"), sem("in_vec"), sem("in_sel"), sem("in_ctx")
        in_attn = [sem(f"in_attn{i}") for i in range(4)]
        in_x, in_xt = sem("in_x"), sem("in_xt")
        in_w = [sem(f"in_w{s}") for s in range(4)]
        pads_done = sem("pads_done")
        k_done, k_act, k_dve = sem("k_done"), sem("k_act"), sem("k_dve")
        a_done, a_act, a_dve = sem("a_done"), sem("a_act"), sem("a_dve")
        fold_done, fold_read = sem("fold_done"), sem("fold_read")
        small_hi_done, small_lo_done = sem("small_hi_done"), sem("small_lo_done")
        whi_done, wlo_done = sem("whi_done"), sem("wlo_done")
        a_hi_done, a_lo_done = sem("a_hi_done"), sem("a_lo_done")
        vw_hi_done, vw_lo_done = sem("vw_hi_done"), sem("vw_lo_done")
        ln1_step, var1_done, rstd1_done, xn1_done = sem("ln1_step"), sem("var1_done"), sem("rstd1_done"), sem("xn1_done")
        ln2_step, var2_done, rstd2_done, xn2_done = sem("ln2_step"), sem("var2_done"), sem("rstd2_done"), sem("xn2_done")
        x1t_done, x1_hi_done, x1_lo_done = sem("x1t_done"), sem("x1_hi_done"), sem("x1_lo_done")
        scores_done, max_done, shift_done, exp_done = sem("scores_done"), sem("max_done"), sem("shift_done"), sem("exp_done")
        sum_done, rinv_done, norm_done = sem("sum_done"), sem("rinv_done"), sem("norm_done")
        pt_done, pt_hi_done, pt_lo_done, pv_done = sem("pt_done"), sem("pt_hi_done"), sem("pt_lo_done"), sem("pv_done")
        x2t_done, x2n_done = sem("x2t_done"), sem("x2n_done")
        x2tr_done, x2_hi_done, x2_lo_done = sem("x2tr_done"), sem("x2_hi_done"), sem("x2_lo_done")
        logits_done, logits_read, top_step = sem("logits_done"), sem("logits_read"), sem("top_step")
        gap_done, egap_done, w16_done, wt_done, wt_read = (
            sem("gap_done"), sem("egap_done"), sem("w16_done"), sem("wt_done"), sem("wt_read"))
        wb_done, wb_read = sem("wb_done"), sem("wb_read")
        up_done, relu_done, h_hi_done, h_lo_done = sem("up_done"), sem("relu_done"), sem("h_hi_done"), sem("h_lo_done")
        down_done, y_done, acc_done, out_done = sem("down_done"), sem("y_done"), sem("acc_done"), sem("out_done")

        def half_heads(tile_ap, s):
            return tile_ap[:, s * SW:(s + 1) * SW].rearrange("p (h j) -> p h j", j=NK)

        scores_ps = ps[:, SC:SC + 2, 0:SW // 2].rearrange("p k (h j) -> p k h j", j=NK)

        def by_bank(per_head):
            return per_head.rearrange("p (k h) -> p k h", k=2)

        def fold_bank(n):
            return HP + n % 4

        block = ctx.enter_context(nc.Block())

        @block.sync
        def _(sp):
            sp.dma_start(raw[:, 0, :], w_attn[0]).then_inc(in_attn[0], 16)
            sp.dma_start(raw[:, 1, :], w_attn[1]).then_inc(in_attn[1], 16)
            sp.dma_start(raw[:, 2, :], w_attn[2]).then_inc(in_attn[2], 16)
            sp.dma_start(raw[:, 3, :], w_attn[3]).then_inc(in_attn[3], 16)
            sp.dma_start(x2t[:], x_t[0:P, :]).then_inc(in_xt, 16)
            sp.dma_start(sel_raw[:], sel).then_inc(in_sel, 16)
            sp.wait_ge(xn1_done, 1)
            sp.dma_start(xin[:], x_nat[P:2 * P, :]).then_inc(in_x, 16)
            for e in range(NE):
                if e == 0:
                    sp.wait_ge(k_done, 8)
                elif e == 1:
                    sp.wait_ge(a_done, H)
                elif e == 2:
                    sp.wait_ge(fold_done, 8)
                elif e == 3:
                    sp.wait_ge(fold_done, 8 + H)
                else:
                    sp.wait_ge(wlo_done, e - 3)
                sp.dma_start(raw[:, e % 4, 0:FF], w1[e]).then_inc(in_w[e % 4], 16)
                sp.dma_start(raw[:, e % 4, FF:2 * FF], w2[e]).then_inc(in_w[e % 4], 16)

            def store(f):
                sp.wait_ge(acc_done, 2 + NE * (f + 1))
                sp.dma_start(out[bass.ds(f * P, P), :], acc[:]).then_inc(out_done, 16)

            sp.sem_inc(out_done, 16)
            with sp.Fori(1, NB) as b:
                sp.wait_ge(xn1_done, b + 1)
                sp.dma_start(xin[:], x_nat[bass.ds((b + 1) % NB * P, P), :]).then_inc(in_x, 16)
                sp.wait_ge(acc_done, 2 + NE * (b - 1) + 1)
                sp.dma_start(x2t[:], x_t[bass.ds(b * P, P), :]).then_inc(in_xt, 16)
                store(b - 1)
            store(NB - 1)
            sp.wait_ge(out_done, 16 * (NB + 1))

        @block.tensor
        def _(pe):
            def product(o, hi, lo, rhs_hi, rhs_lo, start, stop):
                nc.tensor.matmul(o, hi, rhs_hi, start=start, stop=False)
                nc.tensor.matmul(o, hi, rhs_lo, start=False, stop=False)
                return nc.tensor.matmul(o, lo, rhs_hi, start=False, stop=stop)

            pe.wait_ge(in_ctx, 16)
            pe.wait_ge(in_attn[0], 16)
            for n in range(8):
                nc.tensor.matmul(ps[:, n, 0:NB * NK], raw[:, 0, n * P:(n + 1) * P], ctx_sb[:],
                                 start=True, stop=True).then_inc(k_done, 1)
            pe.wait_ge(in_attn[1], 16)
            for h in range(H):
                half = slice(h % 2 * DH, h % 2 * DH + DH)
                n = h // 2
                if h < 8:
                    pe.wait_ge(k_act, h // 2 + 1)
                    pe.wait_ge(k_dve, (h + 1) // 2)
                else:
                    pe.wait_ge(k_act, 4)
                    pe.wait_ge(k_dve, 4)
                    pe.wait_ge(a_act if h % 2 == 0 else a_dve, (h - 8) // 2 + 1)
                nc.tensor.matmul(ps[:, h % 8, 0:NB * NK], raw[half, 1, n * P:(n + 1) * P], k_t[half, n, :],
                                 start=True, stop=True).then_inc(a_done, 1)
            pe.wait_ge(a_act, 8)
            pe.wait_ge(a_dve, 8)

            def fold(n):
                need(pe, fold_read, n - 3)
                if n < 8:
                    if n == 0:
                        pe.wait_ge(in_attn[2], 16)
                    mm = nc.tensor.matmul(ps[:, fold_bank(n), 0:NB * NK], raw[:, 2, n * P:(n + 1) * P], ctx_sb[:],
                                          start=True, stop=True)
                elif n < 8 + H:
                    h = n - 8
                    if h == 0:
                        pe.wait_ge(in_attn[3], 16)
                        pe.wait_ge(fold_read, 8)
                    half = slice(h % 2 * DH, h % 2 * DH + DH)
                    mm = nc.tensor.matmul(ps[:, fold_bank(n), 0:NB * NK], raw[half, 3, h // 2 * P:(h // 2 + 1) * P],
                                          v_t[half, h // 2, :], start=True, stop=True)
                else:
                    b, g = divmod(n - 8 - H, len(GROUPS))
                    if n == 8 + H:
                        pe.wait_ge(fold_read, 8 + H)
                        pe.wait_ge(pads_done, 2)
                    c0, c1 = GROUPS[g]
                    for c in range(c0, c1):
                        mm = nc.tensor.transpose(ps[:, fold_bank(n), (c - c0) * P:(c - c0 + 1) * P],
                                                 vwt[:, b, c * P:(c + 1) * P], ident)
                mm.then_inc(fold_done, 1)

            def turn1(k):
                pe.wait_ge(xn1_done, k + 1)
                for t in range(NT):
                    mm = nc.tensor.transpose(ps[:, TR, t * P:(t + 1) * P], xn1[:, t, :], ident)
                mm.then_inc(x1t_done, 1)

            def scores(b, u):
                t, s = divmod(u, 2)
                if u == 0:
                    pe.wait_ge(x1_lo_done, b + 1)
                    pe.wait_ge(a_lo_done, b + 1)
                need(pe, shift_done, NS * b + u)
                toks = slice(t * P, (t + 1) * P)
                for k in range(2):
                    cols = slice(s * SW + k * SW // 2, s * SW + (k + 1) * SW // 2)
                    mm = product(ps[:, SC + k, 0:SW // 2], x1_hi[:, toks], x1_lo[:, toks], a_hi[:, cols],
                                 a_lo[:, cols], True, True)
                mm.then_inc(scores_done, 1)

            def attention(b, q, table, f):
                for u in steps_at(table, "scores", q):
                    scores(b, u)
                for n in steps_at(table, "turn", q):
                    t, g = divmod(n, len(GROUPS))
                    if g == 0:
                        pe.wait_ge(norm_done, NS * b + 2 * t + 1)
                    if g == 1:
                        pe.wait_ge(norm_done, NS * b + 2 * t + 2)
                    bank_before("turn", n, b, q, table, f)
                    c0, c1 = GROUPS[g]
                    for c in range(c0, c1):
                        mm = nc.tensor.transpose(ps[:, TR, (c - c0) * P:(c - c0 + 1) * P],
                                                 e_sb[:, t % 2, c * P:(c + 1) * P], ident)
                    mm.then_inc(pt_done, 1)
                for pair in steps_at(table, "project", q):
                    pe.wait_ge(pt_lo_done, 12 * b + 6 * (pair + 1))
                    pe.wait_ge(vw_lo_done, b + 1)
                    if f is not None:
                        pe.wait_ge(wb_read, 1 + NE * f + sum(w < q for w in table["spread"]))
                    need(pe, x2t_done, 2 * b + pair)
                    for c in range(NC):
                        cols = slice(c * P, (c + 1) * P)
                        mm = product(ps[:, PV, pair * 2 * P:(pair + 1) * 2 * P], vw_hi[:, cols], vw_lo[:, cols],
                                     pt_hi[:, c, :], pt_lo[:, c, :], c == 0, c == NC - 1)
                    mm.then_inc(pv_done, 1)
                for pair in steps_at(table, "back", q):
                    pe.wait_ge(x2t_done, 2 * b + pair + 1)
                    bank_before("back", pair, b, q, table, f)
                    for t in (2 * pair, 2 * pair + 1):
                        mm = nc.tensor.transpose(ps[:, TR, t * P:(t + 1) * P], x2t[:, t * P:(t + 1) * P], ident)
                    mm.then_inc(x2n_done, 1)
                for _ in steps_at(table, "turn1", q):
                    bank_before("turn1", 0, b, q, table, f)
                    turn1(b + 1)

            users = ("turn", "back", "turn1", "turn_w")

            def bank_before(user, n, b, q, table, f):
                def before(other):
                    if other == user:
                        return n
                    inside = users.index(other) < users.index(user)
                    return sum(a < q or (a == q and inside) for a in table.get(other, ()))

                if b is not None:
                    need(pe, pt_lo_done, 12 * b + before("turn"))
                    need(pe, xn2_done, 2 * b + before("back"))
                    if before("turn1"):
                        pe.wait_ge(x1_lo_done, b + 2)
                if f is None:
                    pe.wait_ge(x1_lo_done, 1)
                else:
                    pe.wait_ge(x2_lo_done, f + 1)
                    if before("turn_w"):
                        pe.wait_ge(wt_read, f + 1)

            def enter(f):
                pe.wait_ge(xn2_done, 2 * f + 2)
                for t in range(NT):
                    mm = nc.tensor.transpose(ps[:, TR, t * P:(t + 1) * P], xn2[:, t, :], ident)
                mm.then_inc(x2tr_done, 1)

            def logits(f):
                pe.wait_ge(x2_lo_done, f + 1)
                pe.wait_ge(x2t_done, 2 * f + 2)
                pe.wait_ge(wb_read, 1 + NE * f)
                for t in range(NT):
                    toks = slice(t * P, (t + 1) * P)
                    mm = product(ps[:, PV, t * NE:(t + 1) * NE], x2_hi[:, toks], x2_lo[:, toks],
                                 wr_hi[:], wr_lo[:], True, True)
                mm.then_inc(logits_done, 1)

            def experts(f, q, together):
                table = MAIN
                if q in table["turn_w"]:
                    pe.wait_ge(w16_done, f + 1)
                    bank_before("turn_w", 0, f + 1 if together else None, q, table, f)
                    for t in range(NT):
                        mm = nc.tensor.transpose(ps[0:2 * NE, TR, t * P:(t + 1) * P], w16[:, t, :], ident)
                    mm.then_inc(wt_done, 1)
                for e in steps_at(table, "spread", q):
                    if e == 0:
                        pe.wait_ge(wt_read, f + 1)
                        pe.wait_ge(logits_read, f + 1)
                    pe.wait_ge(wb_read, 1 + NE * f + e)
                    pairs = sum(p <= q for p in table["project"])
                    if together and pairs:
                        pe.wait_ge(x2t_done, 2 * f + 2 + pairs)
                    nc.tensor.matmul(ps[:, PV, :], sel_r[:, e * P:(e + 1) * P], wt_r[:],
                                     start=True, stop=True).then_inc(wb_done, 1)
                if q < NU:
                    pe.wait_ge(relu_done, 2 + NU * f + q - 1)
                    e, k = divmod(q, FB)
                    cols = slice(e * 2 * FF + k * P, e * 2 * FF + (k + 1) * P)
                    product(ps[:, HP + q % 2, :], w_hi[:, cols], w_lo[:, cols], x2_hi[:], x2_lo[:],
                            True, True).then_inc(up_done, 1)
                if LAG <= q < NU + LAG:
                    u = q - LAG
                    e, k = divmod(u, FB)
                    pe.wait_ge(h_lo_done, 2 + NU * f + u + 1)
                    if k == 0:
                        pe.wait_ge(y_done, 2 + NE * f + e - 1)
                    cols = slice((e * 2 + 1) * FF + k * P, (e * 2 + 1) * FF + (k + 1) * P)
                    product(ps[:, YP + e % 2, :], w_hi[:, cols], w_lo[:, cols], h_hi[:, u % 4, :], h_lo[:, u % 4, :],
                            k == 0, k == FB - 1).then_inc(down_done, 1)

            pe.wait_ge(in_con, 16)
            turn1(0)
            for q in range(SLOTS):
                attention(0, q, FIRST, None)
                for n in folds_at(FIRST, q):
                    fold(n)
            pe.wait_ge(fold_read, FOLDS)
            pe.wait_ge(small_hi_done, 2)
            pe.wait_ge(small_lo_done, 1)
            pe.wait_ge(wlo_done, NE)
            pe.sem_inc(down_done, 4)
            pe.sem_inc(wb_done, 1)
            pe.sem_inc(wt_done, 1)
            with pe.Fori(1, NB) as b:
                scores(b, 0)
                enter(b - 1)
                scores(b, 1)
                logits(b - 1)
                for q in range(SLOTS):
                    attention(b, q, MAIN, b - 1)
                    experts(b - 1, q, True)
            enter(NB - 1)
            logits(NB - 1)
            for q in range(SLOTS):
                experts(NB - 1, q, False)

        @block.scalar
        def _(act):
            act.dma_start(ctx_sb[:], ctx_t).then_inc(in_ctx, 16)
            act.dma_start(xin[:], x_nat[0:P, :]).then_inc(in_x, 16)
            act.dma_start(con[:], consts).then_inc(in_con, 16)
            act.dma_start(vec[:], vecs).then_inc(in_vec, 16)
            for n in range(0, 8, 2):
                act.wait_ge(k_done, n + 1)
                nc.scalar.activation(k_t[:, n, :], ps[:, n, 0:NB * NK], ACT.Copy).then_inc(k_act, 1)
            by_batch = a_all[:].rearrange("p (b n) -> p b n", b=NB)
            for h in range(0, H, 2):
                act.wait_ge(a_done, h + 1)
                nc.scalar.activation(by_batch[:, :, h * NK:(h + 1) * NK],
                                     ps[:, h % 8, 0:NB * NK].rearrange("p (b j) -> p b j", b=NB),
                                     ACT.Copy).then_inc(a_act, 1)

            def fold(n):
                act.wait_ge(fold_done, n + 1)
                if n < 8:
                    ins = nc.scalar.activation(v_t[:, n, :], ps[:, fold_bank(n), 0:NB * NK], ACT.Copy)
                elif n < 8 + H:
                    h = n - 8
                    ins = nc.scalar.activation(
                        vwt[:, :, h * NK:(h + 1) * NK],
                        ps[:, fold_bank(n), 0:NB * NK].rearrange("p (b j) -> p b j", b=NB), ACT.Copy)
                else:
                    b, g = divmod(n - 8 - H, len(GROUPS))
                    c0, c1 = GROUPS[g]
                    ins = nc.scalar.activation(vw_all[:, b * HJP + c0 * P:b * HJP + c1 * P],
                                               ps[:, fold_bank(n), 0:(c1 - c0) * P], ACT.Copy)
                ins.then_inc(fold_read, 1)

            def split_a(k, batch):
                need(act, scores_done, NS * k)
                nc.scalar.activation(a_hi[:], a_all[:, bass.ds(batch * HJ, HJ)], ACT.Copy).then_inc(a_hi_done, 1)

            def turn1(k):
                act.wait_ge(x1t_done, k + 1)
                need(act, scores_done, NS * k)
                nc.scalar.activation(x1_hi[:], ps[:, TR, :], ACT.Copy).then_inc(x1_hi_done, 1)

            def attention(b, q, table):
                for _ in steps_at(table, "split_v", q):
                    need(act, pv_done, 2 * b)
                    if isinstance(b, int):
                        act.wait_ge(fold_read, FOLDS)
                    nc.scalar.activation(vw_hi[:], vw_all[:, bass.ds(b * HJP, HJP)], ACT.Copy).then_inc(vw_hi_done, 1)
                for u in steps_at(table, "exp", q):
                    t, s = divmod(u, 2)
                    act.wait_ge(shift_done, NS * b + u + 1)
                    cols = e_sb[:, t % 2, s * SW:(s + 1) * SW]
                    nc.scalar.activation(cols, cols, ACT.Exp, scale=SCALE).then_inc(exp_done, 1)
                for n in steps_at(table, "turn_hi", q):
                    t, g = divmod(n, len(GROUPS))
                    if g == 0:
                        need(act, pv_done, 2 * b + t // 2)
                    act.wait_ge(pt_done, 12 * b + n + 1)
                    c0, c1 = GROUPS[g]
                    nc.scalar.activation(
                        pt_hi[:, c0:c1, t % 2 * P:t % 2 * P + P],
                        ps[:, TR, 0:(c1 - c0) * P].rearrange("p (c t) -> p c t", t=P),
                        ACT.Copy).then_inc(pt_hi_done, 1)
                for _ in steps_at(table, "turn1", q):
                    turn1(b + 1)
                for _ in steps_at(table, "split_a", q):
                    split_a(b + 1, (b + 1) % NB)

            def enter(f):
                act.wait_ge(x2tr_done, f + 1)
                need(act, up_done, NU * f)
                nc.scalar.activation(x2_hi[:], ps[:, TR, :], ACT.Copy).then_inc(x2_hi_done, 1)

            def experts(f, q):
                table = MAIN
                if q in table["top2"]:
                    act.wait_ge(gap_done, f + 1)
                    nc.scalar.activation(egap[:], gap[:], ACT.Exp).then_inc(egap_done, 1)
                if q in table["turn_w"]:
                    act.wait_ge(wt_done, 1 + f + 1)
                    act.wait_ge(wb_done, 1 + NE * f)
                    nc.scalar.activation(wt_r[:], ps[0:2 * NE, TR, :], ACT.Copy).then_inc(wt_read, 1)
                for e in steps_at(table, "spread", q):
                    act.wait_ge(wb_done, 1 + NE * f + e + 1)
                    act.wait_ge(y_done, 2 + NE * f + e - 1)
                    nc.scalar.activation(wb[:, e % 2, :], ps[:, PV, :], ACT.Copy).then_inc(wb_read, 1)
                if q < NU:
                    act.wait_ge(up_done, NU * f + q + 1)
                    act.wait_ge(h_lo_done, 2 + NU * f + q - 1)
                    nc.scalar.activation(h32[:, q % 2, :], ps[:, HP + q % 2, :], ACT.Relu,
                                         bias=b1_v[:, q:q + 1]).then_inc(relu_done, 1)
                    act.wait_ge(relu_done, 2 + NU * f + q + 1)
                    act.wait_ge(down_done, 4 + NU * f + q - 3)
                    nc.scalar.activation(h_hi[:, q % 4, :], h32[:, q % 2, :], ACT.Copy).then_inc(h_hi_done, 1)

            act.wait_ge(a_act, 8)
            act.wait_ge(a_dve, 8)
            split_a(0, 0)
            turn1(0)
            act.wait_ge(pads_done, 2)
            for q in range(SLOTS):
                attention(0, q, FIRST)
                for n in folds_at(FIRST, q):
                    fold(n)
                for e in steps_at(FIRST, "experts", q):
                    act.wait_ge(in_w[e % 4], 32 * (e // 4 + 1))
                    if e >= 3:
                        act.wait_ge(fold_done, FOLDS)
                    nc.scalar.activation(w_hi[:, e * 2 * FF:(e + 1) * 2 * FF], raw[:, e % 4, :],
                                         ACT.Copy).then_inc(whi_done, 1)
            act.wait_ge(in_vec, 16)
            nc.scalar.activation(wr_hi[:], wr_v, ACT.Copy).then_inc(small_hi_done, 1)
            act.wait_ge(in_sel, 16)
            nc.scalar.activation(sel_r[:], sel_raw[:], ACT.Copy).then_inc(small_hi_done, 1)
            act.wait_ge(wlo_done, NE)
            act.sem_inc(wb_read, 1)
            act.sem_inc(relu_done, 2)
            with act.Fori(1, NB) as b:
                enter(b - 1)
                for q in range(SLOTS):
                    attention(b, q, MAIN)
                    experts(b - 1, q)
            enter(NB - 1)
            for q in range(SLOTS):
                experts(NB - 1, q)

        @block.vector
        def _(dve):
            for n in range(1, 8, 2):
                dve.wait_ge(k_done, n + 1)
                nc.vector.tensor_copy(k_t[:, n, :], ps[:, n, 0:NB * NK]).then_inc(k_dve, 1)

            def statistics_of(src, tiles, ln, signal, base, var_done):
                t0, t1 = tiles
                for t in range(t0, t1):
                    ins = nc.vector.bn_stats(ln["stats"][:, t, :], src[:, t, :])
                ins.then_inc(signal, 1)
                dve.wait_ge(signal, base + 1)
                even_mean, odd_mean = ln["stats"][:, t0:t1, 1], ln["stats"][:, t0:t1, 4]
                m_dif, m_sum = ln["m_dif"][:, t0:t1], ln["m_sum"][:, t0:t1]
                var_in, var_between = ln["var_in"][:, t0:t1], ln["var_between"][:, t0:t1]
                nc.vector.tensor_tensor(m_dif, even_mean, odd_mean, ALU.subtract)
                nc.vector.tensor_tensor(var_in, ln["stats"][:, t0:t1, 2], ln["stats"][:, t0:t1, 5], ALU.add)
                nc.vector.tensor_tensor(m_sum, even_mean, odd_mean, ALU.add).then_inc(signal, 1)
                dve.wait_ge(signal, base + 2)
                nc.vector.scalar_tensor_tensor(var_between, m_dif, 0.25, m_dif, ALU.mult, ALU.mult)
                nc.vector.tensor_scalar(ln["mean"][:, t0:t1], m_sum, 0.5, None, ALU.mult)
                nc.vector.tensor_scalar(var_in, var_in, 1.0 / D, EPS, ALU.mult, ALU.add).then_inc(signal, 1)
                dve.wait_ge(signal, base + 3)
                nc.vector.tensor_tensor(ln["var"][:, t0:t1], var_in, var_between, ALU.add).then_inc(var_done, 1)

            def normalise(dst, src, tiles, ln, signal):
                for t in range(*tiles):
                    ins = nc.vector.tensor_scalar(dst[:, t, :], src[:, t, :], ln["mean"][:, t:t + 1],
                                                  ln["rstd"][:, t:t + 1], ALU.subtract, ALU.mult)
                ins.then_inc(signal, 1)

            def layernorm1(k):
                dve.wait_ge(in_x, 16 * (k + 1))
                statistics_of(xin, (0, NT), ln1, ln1_step, 3 * k, var1_done)
                dve.wait_ge(rstd1_done, k + 1)
                need(dve, x1t_done, k)
                normalise(xn1, xin, (0, NT), ln1, xn1_done)

            def turn1(k):
                dve.wait_ge(x1_hi_done, k + 1)
                nc.vector.tensor_tensor(x1_lo[:], ps[:, TR, :], x1_hi[:].bitcast(F32),
                                        ALU.subtract).then_inc(x1_lo_done, 1)

            x2_natural = ps[:, TR, :].rearrange("p (t d) -> p t d", t=NT)

            def ln2_statistics(b, pair):
                dve.wait_ge(x2n_done, 2 * b + pair + 1)
                statistics_of(x2_natural, (2 * pair, 2 * pair + 2), ln2, ln2_step, 6 * b + 3 * pair, var2_done)

            def ln2_normalise(b, pair):
                dve.wait_ge(rstd2_done, 2 * b + pair + 1)
                if pair == 0:
                    need(dve, x2tr_done, b)
                normalise(xn2, x2_natural, (2 * pair, 2 * pair + 2), ln2, xn2_done)

            def maximum(b, u):
                dve.wait_ge(scores_done, NS * b + u + 1)
                nc.vector.tensor_reduce(by_bank(mx[:, u % 2, :]), scores_ps, AX_X, ALU.max).then_inc(max_done, 1)

            def shift(b, u):
                t, s = divmod(u, 2)
                if s == 0:
                    need(dve, pt_done, 12 * b + 3 * (t - 1))
                dve.wait_ge(max_done, NS * b + u + 1)
                nc.vector.tensor_tensor(
                    e_sb[:, t % 2, s * SW:(s + 1) * SW].rearrange("p (k h j) -> p k h j", k=2, j=NK), scores_ps,
                    by_bank(mx[:, s, :]).unsqueeze(3).to_broadcast([P, 2, HS // 2, NK]),
                    ALU.subtract).then_inc(shift_done, 1)

            def attention(b, q, table):
                for u in steps_at(table, "max", q):
                    maximum(b, u)
                for u in steps_at(table, "shift", q):
                    shift(b, u)
                for u in steps_at(table, "sum", q):
                    t, s = divmod(u, 2)
                    dve.wait_ge(exp_done, NS * b + u + 1)
                    nc.vector.tensor_reduce(ssum[:, s, :], half_heads(e_sb[:, t % 2, :], s), AX_X,
                                            ALU.add).then_inc(sum_done, 1)
                    need(dve, norm_done, NS * b + u - 1)
                    dve.wait_ge(sum_done, NS * b + u + 1)
                    nc.vector.reciprocal(rinv[:, s, :], ssum[:, s, :]).then_inc(rinv_done, 1)
                for n in steps_at(table, "turn_lo", q):
                    t, g = divmod(n, len(GROUPS))
                    dve.wait_ge(pt_hi_done, 12 * b + n + 1)
                    c0, c1 = GROUPS[g]
                    cols = slice(t % 2 * P, t % 2 * P + P)
                    nc.vector.tensor_tensor(
                        pt_lo[:, c0:c1, cols], ps[:, TR, 0:(c1 - c0) * P].rearrange("p (c t) -> p c t", t=P),
                        pt_hi[:, c0:c1, cols].bitcast(F32), ALU.subtract).then_inc(pt_lo_done, 1)
                for pair in steps_at(table, "add", q):
                    dve.wait_ge(pv_done, 2 * b + pair + 1)
                    if pair == 0:
                        dve.wait_ge(in_xt, 16 * (b + 1))
                    cols = slice(pair * 2 * P, (pair + 1) * 2 * P)
                    nc.vector.scalar_tensor_tensor(x2t[:, cols], ps[:, PV, cols], bo_v, x2t[:, cols],
                                                   ALU.add, ALU.add).then_inc(x2t_done, 1)
                for pair in steps_at(table, "ln2", q):
                    ln2_statistics(b, pair)
                    if pair == 0:
                        ln2_normalise(b, pair)
                for _ in steps_at(table, "ln1", q):
                    layernorm1(b + 1)
                for _ in steps_at(table, "turn1", q):
                    turn1(b + 1)

            def enter(f):
                dve.wait_ge(x2_hi_done, f + 1)
                nc.vector.tensor_tensor(x2_lo[:], ps[:, TR, :], x2_hi[:].bitcast(F32),
                                        ALU.subtract).then_inc(x2_lo_done, 1)

            TOP_STEPS = 17

            def choose(f, steps):
                def top(ins):
                    steps[0] += 1
                    ins.then_inc(top_step, 1)
                    dve.wait_ge(top_step, TOP_STEPS * f + steps[0])

                dve.wait_ge(logits_done, f + 1)
                nc.vector.tensor_tensor(
                    lg[:], ps[:, PV, 0:NT * NE].rearrange("p (t e) -> p t e", e=NE),
                    br_v.unsqueeze(1).to_broadcast([P, NT, NE]), ALU.add).then_inc(logits_read, 1)
                dve.wait_ge(logits_read, f + 1)
                ranks = rank.unsqueeze(1).to_broadcast([P, NT, NE])
                for k, (values, chosen) in enumerate(((lg, is1), (lg2, is2))):
                    top(nc.vector.tensor_reduce(best[:, k, :], values[:], AX_X, ALU.max))
                    if k == 1:
                        nc.vector.tensor_tensor(gap[:], best[:, 1, :], best[:, 0, :],
                                                ALU.subtract).then_inc(gap_done, 1)
                    top(nc.vector.tensor_tensor(chosen[:], values[:],
                                                best[:, k, :].unsqueeze(2).to_broadcast([P, NT, NE]), ALU.is_equal))
                    top(nc.vector.tensor_tensor(chosen[:], chosen[:], ranks, ALU.mult))
                    top(nc.vector.tensor_reduce(place_of[:, k, :], chosen[:], AX_X, ALU.max))
                    top(nc.vector.tensor_tensor(chosen[:], ranks,
                                                place_of[:, k, :].unsqueeze(2).to_broadcast([P, NT, NE]),
                                                ALU.is_equal))
                    if k == 0:
                        top(nc.vector.scalar_tensor_tensor(lg2[:], is1[:], BELOW_ALL, lg[:], ALU.mult, ALU.add))

            def weigh(f, steps):
                def top(ins):
                    steps[0] += 1
                    ins.then_inc(top_step, 1)
                    dve.wait_ge(top_step, TOP_STEPS * f + steps[0])

                dve.wait_ge(egap_done, f + 1)
                top(nc.vector.tensor_scalar(den[:], egap[:], 1.0, None, ALU.add))
                top(nc.vector.reciprocal(p1[:], den[:]))
                top(nc.vector.tensor_tensor(p2[:], egap[:], p1[:], ALU.mult))
                nc.vector.tensor_tensor(is1[:], is1[:], p1[:].unsqueeze(2).to_broadcast([P, NT, NE]), ALU.mult)
                top(nc.vector.tensor_tensor(is2[:], is2[:], p2[:].unsqueeze(2).to_broadcast([P, NT, NE]), ALU.mult))
                top(nc.vector.tensor_tensor(rw[:], is1[:], is2[:], ALU.add))
                top(nc.vector.tensor_copy(rw_r[:], rw[:]))
                dve.wait_ge(wt_done, 1 + f)
                nc.vector.tensor_copy(w16[:, :, 0:NE], rw_r[:].bitcast(F32))
                nc.vector.tensor_tensor(w16[:, :, NE:2 * NE], rw[:], rw_r[:].bitcast(F32),
                                        ALU.subtract).then_inc(w16_done, 1)
                assert steps[0] == TOP_STEPS

            def experts(f, q, steps):
                table = MAIN
                if q in table["top2"]:
                    weigh(f, steps)
                if q < NU:
                    dve.wait_ge(h_hi_done, NU * f + q + 1)
                    nc.vector.tensor_tensor(h_lo[:, q % 4, :], h32[:, q % 2, :], h_hi[:, q % 4, :].bitcast(F32),
                                            ALU.subtract).then_inc(h_lo_done, 1)
                for e in steps_at(table, "weight", q):
                    dve.wait_ge(down_done, 4 + NU * f + FB * (e + 1))
                    dve.wait_ge(wb_read, 1 + NE * f + e + 1)
                    dve.wait_ge(acc_done, 2 + NE * f + e - 1)
                    nc.vector.scalar_tensor_tensor(ytmp[:, e % 2, :], ps[:, YP + e % 2, :], b2_v[:, e:e + 1],
                                                   wb[:, e % 2, :], ALU.add, ALU.mult).then_inc(y_done, 1)

            layernorm1(0)
            by_batch = a_all[:].rearrange("p (b n) -> p b n", b=NB)
            for h in range(1, H, 2):
                dve.wait_ge(a_done, h + 1)
                nc.vector.tensor_copy(by_batch[:, :, h * NK:(h + 1) * NK],
                                      ps[:, h % 8, 0:NB * NK].rearrange("p (b j) -> p b j", b=NB)
                                      ).then_inc(a_dve, 1)
            turn1(0)
            dve.wait_ge(pads_done, 2)
            dve.wait_ge(in_vec, 16)
            dve.wait_ge(in_con, 16)
            for q in range(SLOTS):
                attention(0, q, FIRST)
            dve.wait_ge(small_hi_done, 1)
            nc.vector.tensor_tensor(wr_lo[:], wr_v, wr_hi[:].bitcast(F32), ALU.subtract).then_inc(small_lo_done, 1)
            dve.sem_inc(h_lo_done, 2)
            dve.sem_inc(y_done, 2)
            with dve.Fori(1, NB) as b:
                steps = [0]
                maximum(b, 0)
                shift(b, 0)
                ln2_normalise(b - 1, 1)
                enter(b - 1)
                maximum(b, 1)
                choose(b - 1, steps)
                for q in range(SLOTS):
                    attention(b, q, MAIN)
                    experts(b - 1, q, steps)
            steps = [0]
            ln2_normalise(NB - 1, 1)
            enter(NB - 1)
            choose(NB - 1, steps)
            for q in range(SLOTS):
                experts(NB - 1, q, steps)

        @block.gpsimd
        def _(pool):
            def rsqrt(ln, tiles, var_done, k, signal):
                t0, t1 = tiles
                pool.wait_ge(var_done, k + 1)
                nc.gpsimd.tensor_tensor(ln["rstd"][:, t0:t1], ln["var"][:, t0:t1], minus_half[:, t0:t1],
                                        ALU.pow).then_inc(signal, 1)

            def split_a(k, batch):
                pool.wait_ge(a_hi_done, k + 1)
                nc.gpsimd.tensor_tensor(a_lo[:], a_all[:, bass.ds(batch * HJ, HJ)], a_hi[:].bitcast(F32),
                                        ALU.subtract).then_inc(a_lo_done, 1)

            def attention(b, q, table):
                for u in steps_at(table, "sum", q):
                    t, s = divmod(u, 2)
                    pool.wait_ge(rinv_done, NS * b + u + 1)
                    probs = half_heads(e_sb[:, t % 2, :], s)
                    nc.gpsimd.tensor_tensor(probs, probs, rinv[:, s, :].unsqueeze(2).to_broadcast([P, HS, NK]),
                                            ALU.mult).then_inc(norm_done, 1)
                for _ in steps_at(table, "split_v", q):
                    pool.wait_ge(vw_hi_done, b + 1)
                    nc.gpsimd.tensor_tensor(vw_lo[:], vw_all[:, bass.ds(b * HJP, HJP)], vw_hi[:].bitcast(F32),
                                            ALU.subtract).then_inc(vw_lo_done, 1)
                for pair in steps_at(table, "ln2", q):
                    rsqrt(ln2, (2 * pair, 2 * pair + 2), var2_done, 2 * b + pair, rstd2_done)
                for _ in steps_at(table, "ln1", q):
                    rsqrt(ln1, (0, NT), var1_done, b + 1, rstd1_done)
                for _ in steps_at(table, "split_a", q):
                    split_a(b + 1, (b + 1) % NB)

            def experts(f, q):
                if q % FB == 3 and q >= 7:
                    e = q // FB - 1
                    pool.wait_ge(y_done, 2 + NE * f + e + 1)
                    if e == 0:
                        pool.wait_ge(out_done, 16 * (f + 1))
                    pool.wait_ge(acc_done, 2 + NE * f + e)
                    nc.gpsimd.tensor_tensor(acc[:], x2t[:] if e == 0 else acc[:], ytmp[:, e % 2, :],
                                            ALU.add).then_inc(acc_done, 1)

            nc.gpsimd.memset(e_sb[:, :, HJ:HJP], 0.0).then_inc(pads_done, 1)
            nc.gpsimd.memset(vwt[:, :, HJ:HJP], 0.0).then_inc(pads_done, 1)
            pool.wait_ge(in_con, 16)
            rsqrt(ln1, (0, NT), var1_done, 0, rstd1_done)
            split_a(0, 0)
            for q in range(SLOTS):
                attention(0, q, FIRST)
                for e in steps_at(FIRST, "experts", q):
                    pool.wait_ge(whi_done, e + 1)
                    nc.gpsimd.tensor_tensor(w_lo[:, e * 2 * FF:(e + 1) * 2 * FF], raw[:, e % 4, :],
                                            w_hi[:, e * 2 * FF:(e + 1) * 2 * FF].bitcast(F32),
                                            ALU.subtract).then_inc(wlo_done, 1)
            pool.sem_inc(acc_done, 2)
            with pool.Fori(1, NB) as b:
                for q in range(SLOTS):
                    attention(b, q, MAIN)
                    experts(b - 1, q)
            for q in range(SLOTS):
                experts(NB - 1, q)


_INPUTS = ("x_nat", "x_t", "ctx_t", "w_attn", "w1", "w2", "vecs", "consts", "sel")


def kernel(x, ctx_1024, L0_xattn_Wq, L0_xattn_Wk, L0_xattn_Wv, L0_xattn_Wo, L0_xattn_bo, L0_ffn_W_router,
           L0_ffn_b_router, L0_ffn_W1, L0_ffn_b1, L0_ffn_W2, L0_ffn_b2):
    import numpy as np
    import concourse.bacc as bacc
    from concourse.bass_utils import run_bass_kernel_spmd

    def rows_on_partitions(w):
        w = np.asarray(w)
        return w.reshape(-1, P, w.shape[-1]).transpose(1, 0, 2).reshape(P, -1)

    x = np.asarray(x)
    b1 = np.asarray(L0_ffn_b1).reshape(NU, P).T
    b2 = np.asarray(L0_ffn_b2).T
    bo = np.asarray(L0_xattn_bo).reshape(P, 1)
    br = np.broadcast_to(np.asarray(L0_ffn_b_router), (P, NE))
    ones = np.float32(1)
    select = np.zeros((2 * NE, NE * P), np.float32)
    for e in range(NE):
        select[e, e * P:(e + 1) * P] = ones
        select[NE + e, e * P:(e + 1) * P] = ones
    consts = np.concatenate([np.eye(P, dtype=np.float32), np.tile(np.arange(NE, 0, -1, dtype=np.float32), (P, 1)),
                             np.full((P, NT), -0.5, np.float32)], 1)
    data = {
        "x_nat": x.reshape(NB, NT, P, D).transpose(0, 2, 1, 3).reshape(NB * P, NT * D),
        "x_t": x.transpose(0, 2, 1).reshape(NB * P, NQ),
        "ctx_t": np.asarray(ctx_1024).reshape(NB * NK, D).T,
        "w_attn": np.stack([np.asarray(L0_xattn_Wk).T, rows_on_partitions(L0_xattn_Wq), np.asarray(L0_xattn_Wv).T,
                            rows_on_partitions(np.asarray(L0_xattn_Wo).T)]),
        "w1": np.asarray(L0_ffn_W1),
        "w2": np.stack([rows_on_partitions(w) for w in np.asarray(L0_ffn_W2)]),
        "vecs": np.concatenate([b1, b2, bo, br, np.asarray(L0_ffn_W_router)], 1),
        "consts": consts,
        "sel": select,
    }
    nc = bacc.Bacc("TRN2", target_bir_lowering=False, num_devices=1)
    arrays, args = {}, []
    for name in _INPUTS:
        a = np.ascontiguousarray(data[name])
        arrays[f"in_{name}"] = a
        args.append(nc.dram_tensor(f"in_{name}", a.shape, mybir.dt.from_np(a.dtype), kind="ExternalInput").ap())
    out = nc.dram_tensor("out_t", (NB * P, NQ), F32, kind="ExternalOutput").ap()
    xattn_moe_kernel(nc, *args, out)
    got = run_bass_kernel_spmd(nc, [arrays], core_ids=[0]).results[0]["out_t"]
    return got.reshape(NB, D, NQ).transpose(0, 2, 1)
```

```python
from contextlib import ExitStack

import concourse.bass as bass
from concourse import mybir

P = 128
ALU = mybir.AluOpType
ACT = mybir.ActivationFunctionType
F32 = mybir.dt.float32
R32 = mybir.dt.float32r
AX_X = mybir.AxisListType.X

NB, NQ, D = 4, 512, 128
NK = 77
H, DH = 16, 64
NE, FF = 8, 512
EPS = 1e-5
BELOW_ALL = -1e38
SCALE = DH ** -0.5

NT = NQ // P
HJ = H * NK
NC = -(-HJ // P)
HJP = NC * P
VH = HJP // 2
FB = FF // P
NU = NE * FB
BANK = 512

WV, WO, WK, WQ = range(4)

SC, TR, PV, HP, YP = 0, 2, 3, 4, 6
NS = 2 * NT
AHEAD = 2
HS = H // 2
SW = HS * NK
GROUPS = ((0, 4), (4, 8), (8, NC))
V_FOLDS = 8 + H + NB * len(GROUPS)
FOLDS = V_FOLDS + 8 + H

LAG = 4
POOLS_UNIT = 2
TOP_PARTS = 19
SLOTS = NU + LAG + 1
MAIN = {
    "scores": (0, 4, 7, 10, 14, 17, 26, 31),
    "shift": (1, 4, 8, 12, 15, 18, 28, 31),
    "exp": (2, 7, 10, 15, 17, 22, 31, 32),
    "sum": (2, 9, 11, 14, 21, 21, 31, 34),
    "turn": (0, 6, 8, 11, 13, 14, 18, 20, 21, 25, 26, 28),
    "project": (15, 29),
    "add": (14, 29),
    "back": (16, 30),
    "ln2": (15, 29),
    "ln1": (17,),
    "turn1": (22,),
    "split_a": (18, 21),
    "split_v": (0, 4),
    "top2": (4,),
    "turn_w": (7,),
    "spread": (8, 9, 16, 18, 23, 27, 31, 33),
    "max": (0, 3, 7, 11, 14, 17, 24, 31),
    "turn_hi": (0, 6, 9, 11, 13, 14, 18, 19, 21, 24, 26, 27),
    "turn_lo": (0, 5, 9, 11, 13, 13, 17, 18, 20, 23, 26, 26),
    "weight": (7, 13, 16, 20, 22, 28, 33, 33),
    "ln2n": (16, 30),
    "enter": (32,),
    "logits": (2,),
    "ln1n": (18,),
    "split_a_lo": (17, 25),
    "split_v_lo": (0, 5),
    "top": (1, 1, 1, 1, 1, 1, 2, 2, 2, 2, 2, 3, 3, 4, 4, 4, 4, 5, 5),
    "h_lo_pool": (0, 6, 9, 9, 16, 21, 26, 30),
}
FIRST = {
    "scores": (0, 1, 2, 4, 8, 11, 14, 17, 33, 36),
    "shift": (0, 0, 2, 4, 9, 12, 15, 21, 33, 35),
    "exp": (0, 2, 2, 7, 10, 13, 19, 20, 33, 33),
    "sum": (0, 3, 5, 8, 13, 16, 22, 22, 35, 36),
    "turn": (4, 8, 8, 10, 16, 16, 23, 25, 26, 26, 26, 29),
    "project": (21, 31),
    "add": (22, 30),
    "back": (21, 34),
    "ln2": (22, 33),
    "ln1": (2,),
    "turn1": (27,),
    "split_a": (26, 29),
    "split_v": (16, 16),
    "max": (0, 0, 1, 3, 9, 12, 15, 21, 31, 35),
    "turn_hi": (6, 9, 9, 10, 16, 19, 23, 24, 25, 25, 25, 27),
    "turn_lo": (4, 6, 7, 9, 16, 19, 23, 23, 25, 25, 25, 25),
    "fold": (4, 4, 4, 0, 5, 2, 0, 0, 0, 7, 2, 7, 5, 3, 4, 0, 2, 1, 0, 6, 4),
    "experts": (7, 7, 13, 16, 16, 20, 22, 25, 28, 28, 28, 29, 30, 36, 36, 36),
    "ln2n": (23, 35),
    "lo": (9, 9, 13, 17, 22, 27, 27, 29, 29, 29, 29, 29, 36, 36, 36, 36),
    "ln1n": (11,),
    "split_a_lo": (24, 28),
    "split_v_lo": (18, 18),
}


def need(eng, sem, count):
    if isinstance(count, int) and count <= 0:
        return
    eng.wait_ge(sem, count)


def is_first(b):
    return isinstance(b, int) and b == 0


def steps_at(table, what, q):
    return [n for n, at in enumerate(table.get(what, ())) if at == q]


def score_step(b, n):
    n += 0 if is_first(b) else AHEAD
    return b + n // NS, n % NS


def folds_at(table, q):
    counts = table.get("fold", ())
    return range(sum(counts[:q]), sum(counts[:q + 1])) if q < len(counts) else ()


def xattn_moe_kernel(nc, x_nat, x_t, ctx_t, w_attn, w1, w2, vecs, consts, sel, out):
    with ExitStack() as ctx:
        place = [-(-nc.sbuf_base // 32) * 32]

        def at(name, shape, dt, offset):
            return nc.alloc_sbuf_tensor_at(name, shape, dt, offset=offset)

        def sb(name, shape, dt=F32):
            size = 4
            for n in shape[1:]:
                size *= n
            here = place[0]
            place[0] += -(-size // 32) * 32
            assert place[0] <= nc.sbuf_usable_end, (name, place[0], nc.sbuf_usable_end)
            return at(name, shape, dt, here)

        def offset():
            return place[0]

        w_hi_at = offset()
        w_hi = sb("w_hi", [P, NE * 2 * FF], R32)
        w_lo_at = offset()
        w_lo = sb("w_lo", [P, NE * 2 * FF], R32)
        later = 4 * 3 * 2 * FF
        k_t = at("k_t", [P, 8, NB * NK], F32, w_hi_at + later)
        v_t = at("v_t", [P, 8, NB * NK], F32, w_hi_at + later + 4 * 8 * NB * NK)
        vwt = at("vwt", [P, NB, HJP], F32, w_lo_at + later)
        a_all = sb("a_all", [P, (NB - 1) * HJ])
        a_hi = sb("a_hi", [P, HJ], R32)
        a_lo = sb("a_lo", [P, HJ], R32)
        vw_all = sb("vw_all", [P, NB * HJP])
        vw_hi = sb("vw_hi", [P, HJP], R32)
        vw_lo = sb("vw_lo", [P, HJP], R32)
        pt_hi = sb("pt_hi", [P, NC, 2 * P], R32)
        pt_lo = sb("pt_lo", [P, NC, 2 * P], R32)
        h_at = offset()
        h_hi = sb("h_hi", [P, 4, NQ], R32)
        h_lo = sb("h_lo", [P, 4, NQ], R32)
        raw = at("raw", [P, 4, 2 * FF], F32, h_at)
        h32 = sb("h32", [P, 2, NQ])
        ytmp_at = offset()
        ytmp = sb("ytmp", [P, 2, NQ])
        sel_raw = at("sel_raw", [2 * NE, NE * P], F32, ytmp_at)
        e_sb = sb("e_sb", [P, 2, HJP])
        xn1 = sb("xn1", [P, NT, D])
        xn2 = sb("xn2", [P, NT, D])
        x1_hi = sb("x1_hi", [P, NQ], R32)
        x1_lo = sb("x1_lo", [P, NQ], R32)
        x2_hi = sb("x2_hi", [P, NQ], R32)
        x2_lo = sb("x2_lo", [P, NQ], R32)
        xin = sb("xin", [P, NT, D])
        x2t = sb("x2t", [P, NQ])
        acc_at = offset()
        acc = sb("acc", [P, NQ])
        ctx_sb = at("ctx_sb", [P, NB * NK], F32, acc_at)
        wb = sb("wb", [P, 2, NQ])
        sel_r = sb("sel_r", [2 * NE, NE * P], R32)
        wt_r = sb("wt_r", [2 * NE, NQ], R32)
        con = sb("con", [P, P + NE + NT])
        vec = sb("vec", [P, NU + NE + 1 + 2 * NE])
        wr_hi, wr_lo = sb("wr_hi", [P, NE], R32), sb("wr_lo", [P, NE], R32)
        mx, ssum, rinv = sb("mx", [P, 2, HS]), sb("ssum", [P, 2, HS]), sb("rinv", [P, 2, HS])

        def statistics(k):
            return {n: sb(f"{n}{k}", [P, NT] + ([6] if n == "stats" else []))
                    for n in ("stats", "mean", "m_sum", "m_dif", "var_in", "var_between", "var", "rstd")}

        ln1, ln2 = statistics(1), statistics(2)
        lg, lg2 = sb("lg", [P, NT, NE]), sb("lg2", [P, NT, NE])
        best, place_of = sb("best", [P, 2, NT]), sb("place_of", [P, 2, NT])
        gap, egap = sb("gap", [P, NT]), sb("egap", [P, NT])
        den, p1, p2 = sb("den", [P, NT]), sb("p1", [P, NT]), sb("p2", [P, NT])
        is1, is2 = sb("is1", [P, NT, NE]), sb("is2", [P, NT, NE])
        rw, rw_r = sb("rw", [P, NT, NE]), sb("rw_r", [P, NT, NE], R32)
        w16 = sb("w16", [P, NT, 2 * NE])

        ident, rank, minus_half = con[:, 0:P], con[:, P:P + NE], con[:, P + NE:P + NE + NT]
        b1_v, b2_v, bo_v = vec[:, 0:NU], vec[:, NU:NU + NE], vec[:, NU + NE:NU + NE + 1]
        br_v = vec[:, NU + NE + 1:NU + 2 * NE + 1]
        wr_v = vec[:, NU + 2 * NE + 1:NU + 3 * NE + 1]

        ps = ctx.enter_context(nc.psum_tensor("ps", [P, 8, BANK], F32))

        def sem(name):
            return ctx.enter_context(nc.semaphore(name))

        in_con, in_vec, in_sel, in_ctx = sem("in_con"), sem("in_vec"), sem("in_sel"), sem("in_ctx")
        in_attn = [sem(f"in_attn{i}") for i in range(4)]
        in_x, in_xt = sem("in_x"), sem("in_xt")
        in_w = [sem(f"in_w{s}") for s in range(4)]
        pads_done = sem("pads_done")
        k_done, k_act, k_dve = sem("k_done"), sem("k_act"), sem("k_dve")
        a_done = sem("a_done")
        fold_done, fold_act, fold_dve = sem("fold_done"), sem("fold_act"), sem("fold_dve")
        small_hi_done, small_lo_done = sem("small_hi_done"), sem("small_lo_done")
        whi_done, w1_lo_done, w2_lo_done = sem("whi_done"), sem("w1_lo_done"), sem("w2_lo_done")
        first_hi_done, first_lo_done = sem("first_hi_done"), sem("first_lo_done")
        a_hi_done, a_lo_done = sem("a_hi_done"), sem("a_lo_done")
        vw_hi_done, vw_lo_done = sem("vw_hi_done"), sem("vw_lo_done")
        ln1_step, var1_done, rstd1_done, xn1_done = sem("ln1_step"), sem("var1_done"), sem("rstd1_done"), sem("xn1_done")
        ln2_step, var2_done, rstd2_done, xn2_done = sem("ln2_step"), sem("var2_done"), sem("rstd2_done"), sem("xn2_done")
        x1t_done, x1_hi_done, x1_lo_done = sem("x1t_done"), sem("x1_hi_done"), sem("x1_lo_done")
        scores_done, max_done, shift_done, exp_done = sem("scores_done"), sem("max_done"), sem("shift_done"), sem("exp_done")
        sum_done, rinv_done, norm_done = sem("sum_done"), sem("rinv_done"), sem("norm_done")
        pt_done, pt_hi_done, pt_lo_done, pv_done = sem("pt_done"), sem("pt_hi_done"), sem("pt_lo_done"), sem("pv_done")
        x2t_done, x2n_done = sem("x2t_done"), sem("x2n_done")
        x2tr_done, x2_hi_done, x2_lo_done = sem("x2tr_done"), sem("x2_hi_done"), sem("x2_lo_done")
        logits_done, top_step = sem("logits_done"), sem("top_step")
        egap_done, wt_done, wt_read = sem("egap_done"), sem("wt_done"), sem("wt_read")
        wb_done, wb_read = sem("wb_done"), sem("wb_read")
        up_done, relu_done, h_hi_done = sem("up_done"), sem("relu_done"), sem("h_hi_done")
        h_lo_dve, h_lo_pool = sem("h_lo_dve"), sem("h_lo_pool")
        down_done, y_done, acc_done, out_done = sem("down_done"), sem("y_done"), sem("acc_done"), sem("out_done")

        def half_heads(tile_ap, s):
            return tile_ap[:, s * SW:(s + 1) * SW].rearrange("p (h j) -> p h j", j=NK)

        keys_of_others = a_all[:].rearrange("p (b n) -> p b n", b=NB - 1)

        def first_keys(tile_ap, g):
            s, odd = divmod(g, 2)
            return tile_ap[:, s * SW:(s + 1) * SW].rearrange("p (h o j) -> p h o j", o=2, j=NK)[:, :, odd, :]

        def first_keys_ps(g):
            return ps[:, HP + g, 0:4 * NK].rearrange("p (h j) -> p h j", j=NK)

        scores_ps = ps[:, SC:SC + 2, 0:SW // 2].rearrange("p k (h j) -> p k h j", j=NK)

        def by_bank(per_head):
            return per_head.rearrange("p (k h) -> p k h", k=2)

        def fold_bank(n):
            return HP + n % 4

        def low_parts(f, u):
            if u % 4 == POOLS_UNIT:
                return h_lo_pool, 1 + NU // 4 * f + u // 4 + 1
            behind = u % 4 - (u % 4 > POOLS_UNIT)
            return h_lo_dve, 1 + NU // 4 * 3 * f + u // 4 * 3 + behind + 1

        def folds_read(eng, steps):
            keys = max(steps - V_FOLDS, 0)
            need(eng, fold_act, steps - keys // 2)
            need(eng, fold_dve, keys // 2)

        def turn_bank(b, n):
            if is_first(b):
                return (TR, PV)[n % 2] if n < 6 else HP + n % 4
            return TR

        block = ctx.enter_context(nc.Block())

        @block.sync
        def _(sp):
            sp.dma_start(raw[:, WK, :], w_attn[0]).then_inc(in_attn[WK], 16)
            sp.dma_start(raw[:, WQ, :], w_attn[1]).then_inc(in_attn[WQ], 16)
            sp.dma_start(raw[:, WV, :], w_attn[2]).then_inc(in_attn[WV], 16)
            sp.dma_start(raw[:, WO, :], w_attn[3]).then_inc(in_attn[WO], 16)
            sp.dma_start(x2t[:], x_t[0:P, :]).then_inc(in_xt, 16)
            sp.dma_start(sel_raw[:], sel).then_inc(in_sel, 16)
            sp.wait_ge(xn1_done, 1)
            sp.dma_start(xin[:], x_nat[P:2 * P, :]).then_inc(in_x, 16)
            for e in range(NE):
                if e < 4:
                    sp.wait_ge(fold_done, (8, 8 + H, V_FOLDS + 8, FOLDS)[e])
                else:
                    sp.wait_ge(w1_lo_done, e - 3)
                    sp.wait_ge(w2_lo_done, e - 3)
                sp.dma_start(raw[:, e % 4, 0:FF], w1[e]).then_inc(in_w[e % 4], 16)
                sp.dma_start(raw[:, e % 4, FF:2 * FF], w2[e]).then_inc(in_w[e % 4], 16)

            def store(f):
                sp.wait_ge(acc_done, 2 + NE * (f + 1))
                sp.dma_start(out[bass.ds(f * P, P), :], acc[:]).then_inc(out_done, 16)

            sp.sem_inc(out_done, 16)
            with sp.Fori(1, NB) as b:
                sp.wait_ge(xn1_done, b + 1)
                sp.dma_start(xin[:], x_nat[bass.ds((b + 1) % NB * P, P), :]).then_inc(in_x, 16)
                sp.wait_ge(acc_done, 2 + NE * (b - 1) + 1)
                sp.dma_start(x2t[:], x_t[bass.ds(b * P, P), :]).then_inc(in_xt, 16)
                store(b - 1)
            store(NB - 1)
            sp.wait_ge(out_done, 16 * (NB + 1))

        @block.tensor
        def _(pe):
            def product(o, hi, lo, rhs_hi, rhs_lo, start, stop):
                nc.tensor.matmul(o, hi, rhs_hi, start=start, stop=False)
                nc.tensor.matmul(o, hi, rhs_lo, start=False, stop=False)
                return nc.tensor.matmul(o, lo, rhs_hi, start=False, stop=stop)

            def turn1(k):
                pe.wait_ge(xn1_done, k + 1)
                for t in range(NT):
                    mm = nc.tensor.transpose(ps[:, TR, t * P:(t + 1) * P], xn1[:, t, :], ident)
                mm.then_inc(x1t_done, 1)

            pe.wait_ge(in_ctx, 16)
            pe.wait_ge(in_attn[WK], 16)
            for n in range(8):
                mm = nc.tensor.matmul(ps[:, SC + n // 4, n % 4 * NK:(n % 4 + 1) * NK],
                                      raw[:, WK, n * P:(n + 1) * P], ctx_sb[:, 0:NK], start=True, stop=True)
                if n % 4 == 3:
                    mm.then_inc(k_done, 1)
            pe.wait_ge(in_attn[WQ], 16)
            for g in range(4):
                if g < 2:
                    pe.wait_ge(k_act, 1)
                else:
                    pe.wait_ge(k_dve, 1)
                for k in range(4):
                    h = g // 2 * HS + 2 * k + g % 2
                    half = slice(h % 2 * DH, h % 2 * DH + DH)
                    n = h // 2
                    mm = nc.tensor.matmul(ps[:, HP + g, k * NK:(k + 1) * NK], raw[half, WQ, n * P:(n + 1) * P],
                                          k_t[half, n, 0:NK], start=True, stop=True)
                mm.then_inc(a_done, 1)
                if g == 1:
                    pe.wait_ge(in_con, 16)
                    turn1(0)

            def fold(n):
                if n < 4:
                    pe.wait_ge(first_lo_done, n + 1)
                folds_read(pe, n - 3)
                if n < 8:
                    if n == 0:
                        pe.wait_ge(in_attn[WV], 16)
                    mm = nc.tensor.matmul(ps[:, fold_bank(n), 0:NB * NK], raw[:, WV, n * P:(n + 1) * P], ctx_sb[:],
                                          start=True, stop=True)
                elif n < 8 + H:
                    h = n - 8
                    if h == 0:
                        pe.wait_ge(in_attn[WO], 16)
                        folds_read(pe, 8)
                    half = slice(h % 2 * DH, h % 2 * DH + DH)
                    mm = nc.tensor.matmul(ps[:, fold_bank(n), 0:NB * NK], raw[half, WO, h // 2 * P:(h // 2 + 1) * P],
                                          v_t[half, h // 2, :], start=True, stop=True)
                elif n >= V_FOLDS + 8:
                    h = n - V_FOLDS - 8
                    if h == 0:
                        folds_read(pe, V_FOLDS + 8)
                    half = slice(h % 2 * DH, h % 2 * DH + DH)
                    mm = nc.tensor.matmul(ps[:, fold_bank(n), 0:(NB - 1) * NK],
                                          raw[half, WQ, h // 2 * P:(h // 2 + 1) * P], k_t[half, h // 2, NK:NB * NK],
                                          start=True, stop=True)
                elif n >= V_FOLDS:
                    k = n - V_FOLDS
                    mm = nc.tensor.matmul(ps[:, fold_bank(n), 0:(NB - 1) * NK], raw[:, WK, k * P:(k + 1) * P],
                                          ctx_sb[:, NK:NB * NK], start=True, stop=True)
                else:
                    b, g = divmod(n - 8 - H, len(GROUPS))
                    if n == 8 + H:
                        folds_read(pe, 8 + H)
                        pe.wait_ge(pads_done, 2)
                    c0, c1 = GROUPS[g]
                    for c in range(c0, c1):
                        mm = nc.tensor.transpose(ps[:, fold_bank(n), (c - c0) * P:(c - c0 + 1) * P],
                                                 vwt[:, b, c * P:(c + 1) * P], ident)
                mm.then_inc(fold_done, 1)

            def scores(b, u):
                t, s = divmod(u, 2)
                if u == 0:
                    pe.wait_ge(x1_lo_done, b + 1)
                if is_first(b):
                    pe.wait_ge(first_lo_done, 2 * (min(u, 1) + 1))
                elif u < 2:
                    pe.wait_ge(a_lo_done, 2 * (b - 1) + u + 1)
                need(pe, shift_done, NS * b + u)
                toks = slice(t * P, (t + 1) * P)
                for k in range(2):
                    cols = slice(s * SW + k * SW // 2, s * SW + (k + 1) * SW // 2)
                    mm = product(ps[:, SC + k, 0:SW // 2], x1_hi[:, toks], x1_lo[:, toks], a_hi[:, cols],
                                 a_lo[:, cols], True, True)
                mm.then_inc(scores_done, 1)

            def attention(b, q, table, f):
                for n in steps_at(table, "scores", q):
                    scores(*score_step(b, n))
                for n in steps_at(table, "turn", q):
                    t, g = divmod(n, len(GROUPS))
                    if g == 0:
                        pe.wait_ge(norm_done, NS * b + 2 * t + 1)
                    if g == 1:
                        pe.wait_ge(norm_done, NS * b + 2 * t + 2)
                    if f is None:
                        first_bank_before(n)
                    else:
                        bank_before("turn", n, b, q, table, f)
                    c0, c1 = GROUPS[g]
                    for c in range(c0, c1):
                        mm = nc.tensor.transpose(ps[:, turn_bank(b, n), (c - c0) * P:(c - c0 + 1) * P],
                                                 e_sb[:, t % 2, c * P:(c + 1) * P], ident)
                    mm.then_inc(pt_done, 1)
                for pair in steps_at(table, "project", q):
                    pe.wait_ge(pt_lo_done, 12 * b + 6 * (pair + 1))
                    pe.wait_ge(vw_lo_done, 2 * b + 2)
                    if f is not None:
                        pe.wait_ge(wb_read, 1 + NE * f + sum(w < q for w in table["spread"]))
                    need(pe, x2t_done, 2 * b + pair)
                    for c in range(NC):
                        cols = slice(c * P, (c + 1) * P)
                        mm = product(ps[:, PV, pair * 2 * P:(pair + 1) * 2 * P], vw_hi[:, cols], vw_lo[:, cols],
                                     pt_hi[:, c, :], pt_lo[:, c, :], c == 0, c == NC - 1)
                    mm.then_inc(pv_done, 1)
                for pair in steps_at(table, "back", q):
                    pe.wait_ge(x2t_done, 2 * b + pair + 1)
                    bank_before("back", pair, b, q, table, f)
                    for t in (2 * pair, 2 * pair + 1):
                        mm = nc.tensor.transpose(ps[:, TR, t * P:(t + 1) * P], x2t[:, t * P:(t + 1) * P], ident)
                    mm.then_inc(x2n_done, 1)
                for _ in steps_at(table, "turn1", q):
                    bank_before("turn1", 0, b, q, table, f)
                    turn1(b + 1)

            def first_bank_before(n):
                if n < 2:
                    pe.wait_ge(x1_lo_done, 1)
                elif n < 6:
                    pe.wait_ge(pt_lo_done, n - 1)
                elif n < 10:
                    folds_read(pe, FOLDS)
                else:
                    pe.wait_ge(pt_lo_done, n - 3)

            users = ("turn", "back", "turn1", "turn_w", "enter")

            def bank_before(user, n, b, q, table, f):
                def before(other):
                    if other == user:
                        return n
                    inside = users.index(other) < users.index(user)
                    return sum(a < q or (a == q and inside) for a in table.get(other, ()))

                if f is None:
                    pe.wait_ge(pt_lo_done, min(before("turn"), 5))
                elif b is not None:
                    need(pe, pt_lo_done, 12 * b + before("turn"))
                if b is not None:
                    need(pe, xn2_done, 2 * b + before("back"))
                    if before("turn1"):
                        pe.wait_ge(x1_lo_done, b + 2)
                if f is None:
                    pe.wait_ge(x1_lo_done, 1)
                else:
                    pe.wait_ge(x2_lo_done, f + 1)
                    if before("turn_w"):
                        pe.wait_ge(wt_read, f + 1)

            def enter(f):
                pe.wait_ge(xn2_done, 2 * f + 2)
                for t in range(NT):
                    mm = nc.tensor.transpose(ps[:, TR, t * P:(t + 1) * P], xn2[:, t, :], ident)
                mm.then_inc(x2tr_done, 1)

            def logits(f):
                pe.wait_ge(x2_lo_done, f + 1)
                pe.wait_ge(x2t_done, 2 * f + 2)
                pe.wait_ge(wb_read, 1 + NE * f)
                for t in range(NT):
                    toks = slice(t * P, (t + 1) * P)
                    mm = product(ps[:, PV, t * NE:(t + 1) * NE], x2_hi[:, toks], x2_lo[:, toks],
                                 wr_hi[:], wr_lo[:], True, True)
                mm.then_inc(logits_done, 1)

            def experts(f, q, together):
                table = MAIN
                if q in table["logits"]:
                    logits(f)
                if q in table["turn_w"]:
                    pe.wait_ge(top_step, TOP_PARTS * (f + 1))
                    bank_before("turn_w", 0, f + 1 if together else None, q, table, f)
                    for t in range(NT):
                        mm = nc.tensor.transpose(ps[0:2 * NE, TR, t * P:(t + 1) * P], w16[:, t, :], ident)
                    mm.then_inc(wt_done, 1)
                if together and q in table["enter"]:
                    bank_before("enter", 0, f + 1, q, table, f)
                    enter(f + 1)
                for e in steps_at(table, "spread", q):
                    if e == 0:
                        pe.wait_ge(wt_read, f + 1)
                        pe.wait_ge(top_step, TOP_PARTS * f + 1)
                    pe.wait_ge(wb_read, 1 + NE * f + e)
                    pairs = sum(p <= q for p in table["project"])
                    if together and pairs:
                        pe.wait_ge(x2t_done, 2 * f + 2 + pairs)
                    nc.tensor.matmul(ps[:, PV, :], sel_r[:, e * P:(e + 1) * P], wt_r[:],
                                     start=True, stop=True).then_inc(wb_done, 1)
                if q < NU:
                    if q == 0:
                        pe.wait_ge(x2_lo_done, f + 1)
                    pe.wait_ge(relu_done, 2 + NU * f + q - 1)
                    e, k = divmod(q, FB)
                    cols = slice(e * 2 * FF + k * P, e * 2 * FF + (k + 1) * P)
                    product(ps[:, HP + q % 2, :], w_hi[:, cols], w_lo[:, cols], x2_hi[:], x2_lo[:],
                            True, True).then_inc(up_done, 1)
                if LAG <= q < NU + LAG:
                    u = q - LAG
                    e, k = divmod(u, FB)
                    pe.wait_ge(*low_parts(f, u))
                    if k == 0:
                        pe.wait_ge(y_done, 2 + NE * f + e - 1)
                    cols = slice((e * 2 + 1) * FF + k * P, (e * 2 + 1) * FF + (k + 1) * P)
                    product(ps[:, YP + e % 2, :], w_hi[:, cols], w_lo[:, cols], h_hi[:, u % 4, :], h_lo[:, u % 4, :],
                            k == 0, k == FB - 1).then_inc(down_done, 1)

            for q in range(SLOTS):
                attention(0, q, FIRST, None)
                for n in folds_at(FIRST, q):
                    fold(n)
            folds_read(pe, FOLDS)
            pe.wait_ge(small_hi_done, 2)
            pe.wait_ge(small_lo_done, 1)
            pe.wait_ge(w1_lo_done, NE)
            pe.wait_ge(w2_lo_done, NE)
            pe.sem_inc(down_done, 4)
            pe.sem_inc(wb_done, 1)
            pe.sem_inc(wt_done, 1)
            enter(0)
            with pe.Fori(1, NB) as b:
                for q in range(SLOTS):
                    attention(b, q, MAIN, b - 1)
                    experts(b - 1, q, True)
            for q in range(SLOTS):
                experts(NB - 1, q, False)

        @block.scalar
        def _(act):
            act.dma_start(ctx_sb[:], ctx_t).then_inc(in_ctx, 16)
            act.dma_start(xin[:], x_nat[0:P, :]).then_inc(in_x, 16)
            act.dma_start(con[:], consts).then_inc(in_con, 16)
            act.dma_start(vec[:], vecs).then_inc(in_vec, 16)
            act.wait_ge(k_done, 1)
            nc.scalar.activation(k_t[:, 0:4, 0:NK], ps[:, SC, 0:4 * NK].rearrange("p (n j) -> p n j", j=NK),
                                 ACT.Copy).then_inc(k_act, 1)

            def fold(n):
                act.wait_ge(fold_done, n + 1)
                if n < 8:
                    ins = nc.scalar.activation(v_t[:, n, :], ps[:, fold_bank(n), 0:NB * NK], ACT.Copy)
                elif n < 8 + H:
                    h = n - 8
                    ins = nc.scalar.activation(
                        vwt[:, :, h * NK:(h + 1) * NK],
                        ps[:, fold_bank(n), 0:NB * NK].rearrange("p (b j) -> p b j", b=NB), ACT.Copy)
                elif n >= V_FOLDS + 8:
                    h = n - V_FOLDS - 8
                    ins = nc.scalar.activation(
                        keys_of_others[:, :, h * NK:(h + 1) * NK],
                        ps[:, fold_bank(n), 0:(NB - 1) * NK].rearrange("p (b j) -> p b j", b=NB - 1), ACT.Copy)
                elif n >= V_FOLDS:
                    ins = nc.scalar.activation(k_t[:, n - V_FOLDS, NK:NB * NK],
                                               ps[:, fold_bank(n), 0:(NB - 1) * NK], ACT.Copy)
                else:
                    b, g = divmod(n - 8 - H, len(GROUPS))
                    c0, c1 = GROUPS[g]
                    ins = nc.scalar.activation(vw_all[:, b * HJP + c0 * P:b * HJP + c1 * P],
                                               ps[:, fold_bank(n), 0:(c1 - c0) * P], ACT.Copy)
                ins.then_inc(fold_act, 1)

            def split_first(g):
                act.wait_ge(a_done, g + 1)
                nc.scalar.activation(first_keys(a_hi, g), first_keys_ps(g), ACT.Copy).then_inc(first_hi_done, 1)

            def split_a(k, place, s):
                need(act, scores_done, NS * k)
                if is_first(k - 1):
                    folds_read(act, FOLDS)
                nc.scalar.activation(a_hi[:, s * SW:(s + 1) * SW], a_all[:, bass.ds(place * HJ + s * SW, SW)],
                                     ACT.Copy).then_inc(a_hi_done, 1)

            def turn1(k):
                act.wait_ge(x1t_done, k + 1)
                need(act, scores_done, NS * k)
                nc.scalar.activation(x1_hi[:], ps[:, TR, :], ACT.Copy).then_inc(x1_hi_done, 1)

            def attention(b, q, table):
                for s in steps_at(table, "split_v", q):
                    need(act, pv_done, 2 * b)
                    if is_first(b):
                        act.wait_ge(fold_act, V_FOLDS)
                    nc.scalar.activation(vw_hi[:, s * VH:(s + 1) * VH], vw_all[:, bass.ds(b * HJP + s * VH, VH)],
                                         ACT.Copy).then_inc(vw_hi_done, 1)
                for n in steps_at(table, "exp", q):
                    batch, u = score_step(b, n)
                    t, s = divmod(u, 2)
                    act.wait_ge(shift_done, NS * batch + u + 1)
                    cols = e_sb[:, t % 2, s * SW:(s + 1) * SW]
                    nc.scalar.activation(cols, cols, ACT.Exp, scale=SCALE).then_inc(exp_done, 1)
                for n in steps_at(table, "turn_hi", q):
                    t, g = divmod(n, len(GROUPS))
                    if g == 0:
                        need(act, pv_done, 2 * b + t // 2)
                    act.wait_ge(pt_done, 12 * b + n + 1)
                    c0, c1 = GROUPS[g]
                    nc.scalar.activation(
                        pt_hi[:, c0:c1, t % 2 * P:t % 2 * P + P],
                        ps[:, turn_bank(b, n), 0:(c1 - c0) * P].rearrange("p (c t) -> p c t", t=P),
                        ACT.Copy).then_inc(pt_hi_done, 1)
                for _ in steps_at(table, "turn1", q):
                    turn1(b + 1)
                for s in steps_at(table, "split_a", q):
                    split_a(b + 1, b % (NB - 1), s)

            def enter(f):
                act.wait_ge(x2tr_done, f + 1)
                need(act, up_done, NU * f)
                nc.scalar.activation(x2_hi[:], ps[:, TR, :], ACT.Copy).then_inc(x2_hi_done, 1)

            def experts(f, q, together):
                table = MAIN
                if together and q in table["enter"]:
                    enter(f + 1)
                if q in table["top2"]:
                    act.wait_ge(top_step, TOP_PARTS * f + 9)
                    nc.scalar.activation(egap[:], gap[:], ACT.Exp).then_inc(egap_done, 1)
                if q in table["turn_w"]:
                    act.wait_ge(wt_done, 1 + f + 1)
                    act.wait_ge(wb_done, 1 + NE * f)
                    nc.scalar.activation(wt_r[:], ps[0:2 * NE, TR, :], ACT.Copy).then_inc(wt_read, 1)
                for e in steps_at(table, "spread", q):
                    act.wait_ge(wb_done, 1 + NE * f + e + 1)
                    act.wait_ge(y_done, 2 + NE * f + e - 1)
                    nc.scalar.activation(wb[:, e % 2, :], ps[:, PV, :], ACT.Copy).then_inc(wb_read, 1)
                if q < NU:
                    act.wait_ge(up_done, NU * f + q + 1)
                    act.wait_ge(*low_parts(f, q - 2))
                    nc.scalar.activation(h32[:, q % 2, :], ps[:, HP + q % 2, :], ACT.Relu,
                                         bias=b1_v[:, q:q + 1]).then_inc(relu_done, 1)
                    act.wait_ge(relu_done, 2 + NU * f + q + 1)
                    act.wait_ge(down_done, 4 + NU * f + q - 3)
                    nc.scalar.activation(h_hi[:, q % 4, :], h32[:, q % 2, :], ACT.Copy).then_inc(h_hi_done, 1)

            split_first(0)
            split_first(1)
            turn1(0)
            split_first(2)
            split_first(3)
            act.wait_ge(pads_done, 2)
            for q in range(SLOTS):
                attention(0, q, FIRST)
                for n in folds_at(FIRST, q):
                    if n < V_FOLDS or n % 2 == 0:
                        fold(n)
                for n in steps_at(FIRST, "experts", q):
                    e, layer = divmod(n, 2)
                    act.wait_ge(in_w[e % 4], 32 * (e // 4 + 1))
                    if e >= 3:
                        act.wait_ge(fold_done, FOLDS)
                    nc.scalar.activation(w_hi[:, n * FF:(n + 1) * FF], raw[:, e % 4, layer * FF:(layer + 1) * FF],
                                         ACT.Copy).then_inc(whi_done, 1)
            act.wait_ge(in_vec, 16)
            nc.scalar.activation(wr_hi[:], wr_v, ACT.Copy).then_inc(small_hi_done, 1)
            act.wait_ge(in_sel, 16)
            nc.scalar.activation(sel_r[:], sel_raw[:], ACT.Copy).then_inc(small_hi_done, 1)
            act.wait_ge(w1_lo_done, NE)
            act.wait_ge(w2_lo_done, NE)
            act.sem_inc(wb_read, 1)
            act.sem_inc(relu_done, 2)
            enter(0)
            with act.Fori(1, NB) as b:
                for q in range(SLOTS):
                    attention(b, q, MAIN)
                    experts(b - 1, q, True)
            for q in range(SLOTS):
                experts(NB - 1, q, False)

        @block.vector
        def _(dve):
            def statistics_of(src, tiles, ln, signal, base, var_done):
                t0, t1 = tiles
                for t in range(t0, t1):
                    ins = nc.vector.bn_stats(ln["stats"][:, t, :], src[:, t, :])
                ins.then_inc(signal, 1)
                dve.wait_ge(signal, base + 1)
                even_mean, odd_mean = ln["stats"][:, t0:t1, 1], ln["stats"][:, t0:t1, 4]
                m_dif, m_sum = ln["m_dif"][:, t0:t1], ln["m_sum"][:, t0:t1]
                var_in, var_between = ln["var_in"][:, t0:t1], ln["var_between"][:, t0:t1]
                nc.vector.tensor_tensor(m_dif, even_mean, odd_mean, ALU.subtract)
                nc.vector.tensor_tensor(var_in, ln["stats"][:, t0:t1, 2], ln["stats"][:, t0:t1, 5], ALU.add)
                nc.vector.tensor_tensor(m_sum, even_mean, odd_mean, ALU.add).then_inc(signal, 1)
                dve.wait_ge(signal, base + 2)
                nc.vector.scalar_tensor_tensor(var_between, m_dif, 0.25, m_dif, ALU.mult, ALU.mult)
                nc.vector.tensor_scalar(ln["mean"][:, t0:t1], m_sum, 0.5, None, ALU.mult)
                nc.vector.tensor_scalar(var_in, var_in, 1.0 / D, EPS, ALU.mult, ALU.add).then_inc(signal, 1)
                dve.wait_ge(signal, base + 3)
                nc.vector.tensor_tensor(ln["var"][:, t0:t1], var_in, var_between, ALU.add).then_inc(var_done, 1)

            def normalise(dst, src, tiles, ln, signal):
                for t in range(*tiles):
                    ins = nc.vector.tensor_scalar(dst[:, t, :], src[:, t, :], ln["mean"][:, t:t + 1],
                                                  ln["rstd"][:, t:t + 1], ALU.subtract, ALU.mult)
                ins.then_inc(signal, 1)

            def ln1_statistics(k):
                dve.wait_ge(in_x, 16 * (k + 1))
                statistics_of(xin, (0, NT), ln1, ln1_step, 3 * k, var1_done)

            def ln1_normalise(k):
                dve.wait_ge(rstd1_done, k + 1)
                need(dve, x1t_done, k)
                normalise(xn1, xin, (0, NT), ln1, xn1_done)

            def turn1(k):
                dve.wait_ge(x1_hi_done, k + 1)
                nc.vector.tensor_tensor(x1_lo[:], ps[:, TR, :], x1_hi[:].bitcast(F32),
                                        ALU.subtract).then_inc(x1_lo_done, 1)

            x2_natural = ps[:, TR, :].rearrange("p (t d) -> p t d", t=NT)

            def ln2_statistics(b, pair):
                dve.wait_ge(x2n_done, 2 * b + pair + 1)
                statistics_of(x2_natural, (2 * pair, 2 * pair + 2), ln2, ln2_step, 6 * b + 3 * pair, var2_done)

            def ln2_normalise(b, pair):
                dve.wait_ge(rstd2_done, 2 * b + pair + 1)
                if pair == 0:
                    need(dve, x2tr_done, b)
                normalise(xn2, x2_natural, (2 * pair, 2 * pair + 2), ln2, xn2_done)

            def maximum(b, u):
                dve.wait_ge(scores_done, NS * b + u + 1)
                nc.vector.tensor_reduce(by_bank(mx[:, u % 2, :]), scores_ps, AX_X, ALU.max).then_inc(max_done, 1)

            def shift(b, u):
                t, s = divmod(u, 2)
                if s == 0:
                    need(dve, pt_done, 12 * b + 3 * (t - 1))
                dve.wait_ge(max_done, NS * b + u + 1)
                nc.vector.tensor_tensor(
                    e_sb[:, t % 2, s * SW:(s + 1) * SW].rearrange("p (k h j) -> p k h j", k=2, j=NK), scores_ps,
                    by_bank(mx[:, s, :]).unsqueeze(3).to_broadcast([P, 2, HS // 2, NK]),
                    ALU.subtract).then_inc(shift_done, 1)

            def attention(b, q, table):
                for n in range(len(table["max"])):
                    if table["max"][n] == q:
                        maximum(*score_step(b, n))
                    if table["shift"][n] == q:
                        shift(*score_step(b, n))
                for n in steps_at(table, "sum", q):
                    batch, u = score_step(b, n)
                    t, s = divmod(u, 2)
                    dve.wait_ge(exp_done, NS * batch + u + 1)
                    nc.vector.tensor_reduce(ssum[:, s, :], half_heads(e_sb[:, t % 2, :], s), AX_X,
                                            ALU.add).then_inc(sum_done, 1)
                    need(dve, norm_done, NS * batch + u - 1)
                    dve.wait_ge(sum_done, NS * batch + u + 1)
                    nc.vector.reciprocal(rinv[:, s, :], ssum[:, s, :]).then_inc(rinv_done, 1)
                for n in steps_at(table, "turn_lo", q):
                    t, g = divmod(n, len(GROUPS))
                    dve.wait_ge(pt_hi_done, 12 * b + n + 1)
                    c0, c1 = GROUPS[g]
                    cols = slice(t % 2 * P, t % 2 * P + P)
                    nc.vector.tensor_tensor(
                        pt_lo[:, c0:c1, cols], ps[:, turn_bank(b, n), 0:(c1 - c0) * P].rearrange("p (c t) -> p c t", t=P),
                        pt_hi[:, c0:c1, cols].bitcast(F32), ALU.subtract).then_inc(pt_lo_done, 1)
                for pair in steps_at(table, "add", q):
                    dve.wait_ge(pv_done, 2 * b + pair + 1)
                    if pair == 0:
                        dve.wait_ge(in_xt, 16 * (b + 1))
                    cols = slice(pair * 2 * P, (pair + 1) * 2 * P)
                    nc.vector.scalar_tensor_tensor(x2t[:, cols], ps[:, PV, cols], bo_v, x2t[:, cols],
                                                   ALU.add, ALU.add).then_inc(x2t_done, 1)
                for pair in steps_at(table, "ln2", q):
                    ln2_statistics(b, pair)
                for pair in steps_at(table, "ln2n", q):
                    ln2_normalise(b, pair)
                for _ in steps_at(table, "ln1", q):
                    ln1_statistics(b + 1)
                for _ in steps_at(table, "ln1n", q):
                    ln1_normalise(b + 1)
                for _ in steps_at(table, "turn1", q):
                    turn1(b + 1)

            def enter(f):
                dve.wait_ge(x2_hi_done, f + 1)
                nc.vector.tensor_tensor(x2_lo[:], ps[:, TR, :], x2_hi[:].bitcast(F32),
                                        ALU.subtract).then_inc(x2_lo_done, 1)

            def top(f, n):
                need(dve, top_step, TOP_PARTS * f + n)

                def of_tokens(column):
                    return column.unsqueeze(2).to_broadcast([P, NT, NE])

                ranks = rank.unsqueeze(1).to_broadcast([P, NT, NE])
                k = 0 if n < 7 else 1
                values, chosen = ((lg, is1), (lg2, is2))[k]
                if n == 0:
                    dve.wait_ge(logits_done, f + 1)
                    part = nc.vector.tensor_tensor(
                        lg[:], ps[:, PV, 0:NT * NE].rearrange("p (t e) -> p t e", e=NE),
                        br_v.unsqueeze(1).to_broadcast([P, NT, NE]), ALU.add)
                elif n in (1, 7):
                    part = nc.vector.tensor_reduce(best[:, k, :], values[:], AX_X, ALU.max)
                elif n in (2, 8):
                    if k == 1:
                        nc.vector.tensor_tensor(gap[:], best[:, 1, :], best[:, 0, :], ALU.subtract)
                    part = nc.vector.tensor_tensor(chosen[:], values[:], of_tokens(best[:, k, :]), ALU.is_equal)
                elif n in (3, 9):
                    part = nc.vector.tensor_tensor(chosen[:], chosen[:], ranks, ALU.mult)
                elif n in (4, 10):
                    part = nc.vector.tensor_reduce(place_of[:, k, :], chosen[:], AX_X, ALU.max)
                elif n in (5, 11):
                    part = nc.vector.tensor_tensor(chosen[:], ranks, of_tokens(place_of[:, k, :]), ALU.is_equal)
                elif n == 6:
                    part = nc.vector.scalar_tensor_tensor(lg2[:], is1[:], BELOW_ALL, lg[:], ALU.mult, ALU.add)
                elif n == 12:
                    dve.wait_ge(egap_done, f + 1)
                    part = nc.vector.tensor_scalar(den[:], egap[:], 1.0, None, ALU.add)
                elif n == 13:
                    part = nc.vector.reciprocal(p1[:], den[:])
                elif n == 14:
                    part = nc.vector.tensor_tensor(p2[:], egap[:], p1[:], ALU.mult)
                elif n == 15:
                    nc.vector.tensor_tensor(is1[:], is1[:], of_tokens(p1[:]), ALU.mult)
                    part = nc.vector.tensor_tensor(is2[:], is2[:], of_tokens(p2[:]), ALU.mult)
                elif n == 16:
                    part = nc.vector.tensor_tensor(rw[:], is1[:], is2[:], ALU.add)
                elif n == 17:
                    part = nc.vector.tensor_copy(rw_r[:], rw[:])
                elif n == 18:
                    dve.wait_ge(wt_done, 1 + f)
                    nc.vector.tensor_copy(w16[:, :, 0:NE], rw_r[:].bitcast(F32))
                    part = nc.vector.tensor_tensor(w16[:, :, NE:2 * NE], rw[:], rw_r[:].bitcast(F32), ALU.subtract)
                part.then_inc(top_step, 1)

            def experts(f, q, together):
                table = MAIN
                parts = steps_at(table, "top", q)[1:]
                if together and q in table["enter"]:
                    enter(f + 1)
                for n in parts[:1]:
                    top(f, n)
                if q < NU and q % 4 != POOLS_UNIT:
                    dve.wait_ge(h_hi_done, NU * f + q + 1)
                    nc.vector.tensor_tensor(h_lo[:, q % 4, :], h32[:, q % 2, :], h_hi[:, q % 4, :].bitcast(F32),
                                            ALU.subtract).then_inc(h_lo_dve, 1)
                for n in parts[1:2]:
                    top(f, n)
                for e in steps_at(table, "weight", q):
                    dve.wait_ge(down_done, 4 + NU * f + FB * (e + 1))
                    dve.wait_ge(wb_read, 1 + NE * f + e + 1)
                    dve.wait_ge(acc_done, 2 + NE * f + e - 1)
                    nc.vector.scalar_tensor_tensor(ytmp[:, e % 2, :], ps[:, YP + e % 2, :], b2_v[:, e:e + 1],
                                                   wb[:, e % 2, :], ALU.add, ALU.mult).then_inc(y_done, 1)
                for n in parts[2:]:
                    top(f, n)

            ln1_statistics(0)
            dve.wait_ge(k_done, 2)
            nc.vector.tensor_copy(k_t[:, 4:8, 0:NK], ps[:, SC + 1, 0:4 * NK].rearrange("p (n j) -> p n j", j=NK)
                                  ).then_inc(k_dve, 1)
            ln1_normalise(0)
            for g in range(4):
                dve.wait_ge(first_hi_done, g + 1)
                nc.vector.tensor_tensor(first_keys(a_lo, g), first_keys_ps(g), first_keys(a_hi, g).bitcast(F32),
                                        ALU.subtract).then_inc(first_lo_done, 1)
                if g == 1:
                    turn1(0)

            def fold(n):
                dve.wait_ge(fold_done, n + 1)
                if n < V_FOLDS + 8:
                    ins = nc.vector.tensor_copy(k_t[:, n - V_FOLDS, NK:NB * NK], ps[:, fold_bank(n), 0:(NB - 1) * NK])
                else:
                    h = n - V_FOLDS - 8
                    ins = nc.vector.tensor_copy(
                        keys_of_others[:, :, h * NK:(h + 1) * NK],
                        ps[:, fold_bank(n), 0:(NB - 1) * NK].rearrange("p (b j) -> p b j", b=NB - 1))
                ins.then_inc(fold_dve, 1)

            dve.wait_ge(pads_done, 2)
            dve.wait_ge(in_vec, 16)
            dve.wait_ge(in_con, 16)
            for q in range(SLOTS):
                attention(0, q, FIRST)
                for n in folds_at(FIRST, q):
                    if n >= V_FOLDS and n % 2 == 1:
                        fold(n)
                for n in steps_at(FIRST, "lo", q):
                    if n % 2 == 1:
                        dve.wait_ge(whi_done, n + 1)
                        nc.vector.tensor_tensor(w_lo[:, n * FF:(n + 1) * FF], raw[:, n // 2 % 4, FF:2 * FF],
                                                w_hi[:, n * FF:(n + 1) * FF].bitcast(F32),
                                                ALU.subtract).then_inc(w2_lo_done, 1)
            dve.wait_ge(small_hi_done, 1)
            nc.vector.tensor_tensor(wr_lo[:], wr_v, wr_hi[:].bitcast(F32), ALU.subtract).then_inc(small_lo_done, 1)
            dve.sem_inc(h_lo_dve, 1)
            dve.sem_inc(y_done, 2)
            enter(0)
            with dve.Fori(1, NB) as b:
                for q in range(SLOTS):
                    for n in steps_at(MAIN, "top", q)[:1]:
                        top(b - 1, n)
                    attention(b, q, MAIN)
                    experts(b - 1, q, True)
            for q in range(SLOTS):
                for n in steps_at(MAIN, "top", q)[:1]:
                    top(NB - 1, n)
                experts(NB - 1, q, False)

        @block.gpsimd
        def _(pool):
            def rsqrt(ln, tiles, var_done, k, signal):
                t0, t1 = tiles
                pool.wait_ge(var_done, k + 1)
                nc.gpsimd.tensor_tensor(ln["rstd"][:, t0:t1], ln["var"][:, t0:t1], minus_half[:, t0:t1],
                                        ALU.pow).then_inc(signal, 1)

            def split_a(k, place, s):
                cols = slice(s * SW, (s + 1) * SW)
                pool.wait_ge(a_hi_done, 2 * (k - 1) + s + 1)
                nc.gpsimd.tensor_tensor(a_lo[:, cols], a_all[:, bass.ds(place * HJ + s * SW, SW)],
                                        a_hi[:, cols].bitcast(F32), ALU.subtract).then_inc(a_lo_done, 1)

            def attention(b, q, table):
                for n in steps_at(table, "sum", q):
                    batch, u = score_step(b, n)
                    t, s = divmod(u, 2)
                    pool.wait_ge(rinv_done, NS * batch + u + 1)
                    probs = half_heads(e_sb[:, t % 2, :], s)
                    nc.gpsimd.tensor_tensor(probs, probs, rinv[:, s, :].unsqueeze(2).to_broadcast([P, HS, NK]),
                                            ALU.mult).then_inc(norm_done, 1)
                for s in steps_at(table, "split_v_lo", q):
                    cols = slice(s * VH, (s + 1) * VH)
                    pool.wait_ge(vw_hi_done, 2 * b + s + 1)
                    nc.gpsimd.tensor_tensor(vw_lo[:, cols], vw_all[:, bass.ds(b * HJP + s * VH, VH)],
                                            vw_hi[:, cols].bitcast(F32), ALU.subtract).then_inc(vw_lo_done, 1)
                for pair in steps_at(table, "ln2", q):
                    rsqrt(ln2, (2 * pair, 2 * pair + 2), var2_done, 2 * b + pair, rstd2_done)
                for _ in steps_at(table, "ln1", q):
                    rsqrt(ln1, (0, NT), var1_done, b + 1, rstd1_done)
                for s in steps_at(table, "split_a_lo", q):
                    split_a(b + 1, b % (NB - 1), s)

            def experts(f, q):
                for n in steps_at(MAIN, "h_lo_pool", q):
                    u = 4 * n + POOLS_UNIT
                    pool.wait_ge(h_hi_done, NU * f + u + 1)
                    nc.gpsimd.tensor_tensor(h_lo[:, u % 4, :], h32[:, u % 2, :], h_hi[:, u % 4, :].bitcast(F32),
                                            ALU.subtract).then_inc(h_lo_pool, 1)
                if q % FB == 3 and q >= 7:
                    e = q // FB - 1
                    pool.wait_ge(y_done, 2 + NE * f + e + 1)
                    if e == 0:
                        pool.wait_ge(out_done, 16 * (f + 1))
                    pool.wait_ge(acc_done, 2 + NE * f + e)
                    nc.gpsimd.tensor_tensor(acc[:], x2t[:] if e == 0 else acc[:], ytmp[:, e % 2, :],
                                            ALU.add).then_inc(acc_done, 1)

            nc.gpsimd.memset(e_sb[:, :, HJ:HJP], 0.0).then_inc(pads_done, 1)
            nc.gpsimd.memset(vwt[:, :, HJ:HJP], 0.0).then_inc(pads_done, 1)
            pool.wait_ge(in_con, 16)
            rsqrt(ln1, (0, NT), var1_done, 0, rstd1_done)
            for q in range(SLOTS):
                attention(0, q, FIRST)
                for n in steps_at(FIRST, "lo", q):
                    if n % 2 == 0:
                        pool.wait_ge(whi_done, n + 1)
                        nc.gpsimd.tensor_tensor(w_lo[:, n * FF:(n + 1) * FF], raw[:, n // 2 % 4, 0:FF],
                                                w_hi[:, n * FF:(n + 1) * FF].bitcast(F32),
                                                ALU.subtract).then_inc(w1_lo_done, 1)
            pool.sem_inc(h_lo_pool, 1)
            pool.sem_inc(acc_done, 2)
            with pool.Fori(1, NB) as b:
                for q in range(SLOTS):
                    attention(b, q, MAIN)
                    experts(b - 1, q)
            for q in range(SLOTS):
                experts(NB - 1, q)


_INPUTS = ("x_nat", "x_t", "ctx_t", "w_attn", "w1", "w2", "vecs", "consts", "sel")


def kernel(x, ctx_1024, L0_xattn_Wq, L0_xattn_Wk, L0_xattn_Wv, L0_xattn_Wo, L0_xattn_bo, L0_ffn_W_router,
           L0_ffn_b_router, L0_ffn_W1, L0_ffn_b1, L0_ffn_W2, L0_ffn_b2):
    import numpy as np
    import concourse.bacc as bacc
    from concourse.bass_utils import run_bass_kernel_spmd

    def rows_on_partitions(w):
        w = np.asarray(w)
        return w.reshape(-1, P, w.shape[-1]).transpose(1, 0, 2).reshape(P, -1)

    x = np.asarray(x)
    b1 = np.asarray(L0_ffn_b1).reshape(NU, P).T
    b2 = np.asarray(L0_ffn_b2).T
    bo = np.asarray(L0_xattn_bo).reshape(P, 1)
    br = np.broadcast_to(np.asarray(L0_ffn_b_router), (P, NE))
    ones = np.float32(1)
    select = np.zeros((2 * NE, NE * P), np.float32)
    for e in range(NE):
        select[e, e * P:(e + 1) * P] = ones
        select[NE + e, e * P:(e + 1) * P] = ones
    consts = np.concatenate([np.eye(P, dtype=np.float32), np.tile(np.arange(NE, 0, -1, dtype=np.float32), (P, 1)),
                             np.full((P, NT), -0.5, np.float32)], 1)
    data = {
        "x_nat": x.reshape(NB, NT, P, D).transpose(0, 2, 1, 3).reshape(NB * P, NT * D),
        "x_t": x.transpose(0, 2, 1).reshape(NB * P, NQ),
        "ctx_t": np.asarray(ctx_1024).reshape(NB * NK, D).T,
        "w_attn": np.stack([np.asarray(L0_xattn_Wk).T, rows_on_partitions(L0_xattn_Wq), np.asarray(L0_xattn_Wv).T,
                            rows_on_partitions(np.asarray(L0_xattn_Wo).T)]),
        "w1": np.asarray(L0_ffn_W1),
        "w2": np.stack([rows_on_partitions(w) for w in np.asarray(L0_ffn_W2)]),
        "vecs": np.concatenate([b1, b2, bo, br, np.asarray(L0_ffn_W_router)], 1),
        "consts": consts,
        "sel": select,
    }
    nc = bacc.Bacc("TRN2", target_bir_lowering=False, num_devices=1)
    arrays, args = {}, []
    for name in _INPUTS:
        a = np.ascontiguousarray(data[name])
        arrays[f"in_{name}"] = a
        args.append(nc.dram_tensor(f"in_{name}", a.shape, mybir.dt.from_np(a.dtype), kind="ExternalInput").ap())
    out = nc.dram_tensor("out_t", (NB * P, NQ), F32, kind="ExternalOutput").ap()
    xattn_moe_kernel(nc, *args, out)
    got = run_bass_kernel_spmd(nc, [arrays], core_ids=[0]).results[0]["out_t"]
    return got.reshape(NB, D, NQ).transpose(0, 2, 1)
```
